# Optimizing a Trainium2 kernel written in Bass

```python
import numpy as np
import jax
import jax.numpy as jnp

def _softmax(x, axis=-1):
    return jax.nn.softmax(x, axis=axis)

def _gelu(x):
    return jax.nn.gelu(x, approximate=True)

def _silu(x):
    return jax.nn.silu(x)

def _sigmoid(x):
    return jax.nn.sigmoid(x)

def _layernorm(x, axis=-1, eps=1e-05):
    m = jnp.mean(x, axis=axis, keepdims=True)
    v = jnp.var(x, axis=axis, keepdims=True)
    return (x - m) / jnp.sqrt(v + eps)

def _scatter_add(tgt, idx, src, axis=0):
    return tgt.at[idx].add(src)

def _segment_sum(src, seg, n):
    return jax.ops.segment_sum(src, seg, n)
kernel_name = 'mk_rec_standalone_d1_rec_r8_e2b2ad'

def setup_inputs(seed: int=0):
    np.random.seed(seed)
    _w = jnp.asarray

    def _rec_inputs():
        import jax
        import jax.numpy as jnp
        _rk = jax.random.key(seed)
        r_query = -0.00154741 + 1.00114 * jax.random.normal(jax.random.fold_in(_rk, 1), (1024, 128), jnp.float32)
        r_keys = -0.00010897 + 0.999902 * jax.random.normal(jax.random.fold_in(_rk, 2), (1024, 200, 128), jnp.float32)
        r_mask = jax.random.randint(jax.random.fold_in(_rk, 3), (1024, 200), 0, 2, jnp.int32)
        return (r_query, r_keys, r_mask)
    r_query, r_keys, r_mask = _rec_inputs()

    def _L0_rec_setup():
        import jax, jax.numpy as jnp
        import numpy as np
        B, N, D = (256, 200, 128)
        H1, H2 = (256, 128)
        key = jax.random.key(seed)
        ks = jax.random.split(key, 6)
        query = jax.random.normal(ks[0], (B, D), dtype=jnp.float32)
        keys = jax.random.normal(ks[1], (B, N, D), dtype=jnp.float32)
        mask = jax.random.randint(ks[2], (B, N), 0, 2, dtype=jnp.int32)
        W1 = jax.random.normal(ks[3], (4 * D, H1), dtype=jnp.float32) / np.sqrt(4 * D)
        b1 = jnp.zeros((H1,), dtype=jnp.float32)
        W2 = jax.random.normal(ks[4], (H1, H2), dtype=jnp.float32) / np.sqrt(H1)
        b2 = jnp.zeros((H2,), dtype=jnp.float32)
        W3 = jax.random.normal(ks[5], (H2, 1), dtype=jnp.float32) / np.sqrt(H2)
        b3 = jnp.zeros((1,), dtype=jnp.float32)
        return {'query': query, 'keys': keys, 'mask': mask, 'W1': W1, 'b1': b1, 'W2': W2, 'b2': b2, 'W3': W3, 'b3': b3}
    _L0_rec_all = _L0_rec_setup()
    _L0_rec_in = {k: v for k, v in _L0_rec_all.items() if k in ('W1', 'b1', 'W2', 'b2', 'W3', 'b3')}
    del _L0_rec_all
    return {'r_query': r_query, 'r_keys': r_keys, 'r_mask': r_mask, 'L0_rec_W1': _L0_rec_in['W1'], 'L0_rec_b1': _L0_rec_in['b1'], 'L0_rec_W2': _L0_rec_in['W2'], 'L0_rec_b2': _L0_rec_in['b2'], 'L0_rec_W3': _L0_rec_in['W3'], 'L0_rec_b3': _L0_rec_in['b3']}

def reference(r_query, r_keys, r_mask, L0_rec_W1, L0_rec_b1, L0_rec_W2, L0_rec_b2, L0_rec_W3, L0_rec_b3):
    import jax
    import jax.numpy as jnp

    def _L0_rec_ref(query, keys, mask, W1, b1, W2, b2, W3, b3):
        import jax, jax.numpy as jnp
        import numpy as np
        B, N, D = (256, 200, 128)
        H1, H2 = (256, 128)
        q = query[:, None, :]
        qe = jnp.broadcast_to(q, keys.shape)
        att_in = jnp.concatenate([qe, keys, qe - keys, qe * keys], axis=-1)
        h = jax.nn.relu(att_in @ W1 + b1)
        h = jax.nn.relu(h @ W2 + b2)
        scores = (h @ W3 + b3)[..., 0]
        mask_bool = mask > 0
        scores = jnp.where(mask_bool, scores, jnp.float32(-10000.0))
        probs = jax.nn.softmax(scores, axis=-1) * mask_bool.astype(scores.dtype)
        denom = probs.sum(axis=-1, keepdims=True)
        probs = jnp.where(denom > 0, probs / jnp.maximum(denom, 1e-12), jnp.zeros_like(probs))
        user_interest = jnp.einsum('bn,bnd->bd', probs, keys)
        return user_interest
    y = _L0_rec_ref(r_query, r_keys, r_mask, L0_rec_W1, L0_rec_b1, L0_rec_W2, L0_rec_b2, L0_rec_W3, L0_rec_b3)
    return y

_drawn_inputs = setup_inputs


def setup_inputs(seed=0):
    import zlib

    import numpy as np

    out = dict(_drawn_inputs(seed))
    spreads = {'L0_rec_b1': (0.0, 0.1), 'L0_rec_b2': (0.0, 0.1)}
    factors = {}
    for name, (base, spread) in spreads.items():
        noise = np.random.default_rng([zlib.crc32(name.encode()), seed]).standard_normal(out[name].shape)
        drawn = base * np.exp(spread * noise) if base else spread * noise
        out[name] = jnp.asarray(drawn.astype(out[name].dtype))
    for name, factor in factors.items():
        out[name] = (out[name] * factor).astype(out[name].dtype)
    return out
```

```python
from contextlib import ExitStack

import concourse.bass as bass
from concourse import mybir

F32 = mybir.dt.float32
F32R = mybir.dt.float32r
I32 = mybir.dt.int32
ALU = mybir.AluOpType
ACT = mybir.ActivationFunctionType
AX_X = mybir.AxisListType.X

P = 128
MASKED_SCORE = -10000.0
LEAST_DENOMINATOR = 1e-12

PAIRS = 16
GROUPS_PER_ROUND = 2
ROUND = PAIRS * GROUPS_PER_ROUND
CHUNK = 4
LOW_ROW = 64

LAG_LAYER1 = 1
LAG_HIDDEN1 = 1
LAG_LAYER2 = 3
LAG_HIDDEN2 = 3
LAG_HIDDEN2_LOW = 4
LAG_SCORE = 5
LAG_SOFTMAX = PAIRS + 5
LAG_SPREAD = PAIRS + 8

WEIGHT_BUFS = 2
HIDDEN1_BUFS = 4
HIDDEN2_BUFS = 4


def target_attention_kernel(nc, keys_t, query_t, mask, w1, b1, w2, b2, w3_column, w3_row, b3, out):
    n_chunks, _, chunk_columns = keys_t.shape
    n_users = query_t.shape[1]
    N_KEYS = mask.shape[1] // 2
    H1 = w1.shape[1]
    H2 = w2.shape[1]
    HALVES = H1 // P
    W = 2 * N_KEYS
    N_PAIRS = n_users // 2
    N_GROUPS = N_PAIRS // PAIRS
    GROUP_USERS = 2 * PAIRS
    N_ROUNDS = N_PAIRS // ROUND
    CHUNKS_PER_ROUND = ROUND // CHUNK
    CHUNKS_PER_GROUP = PAIRS // CHUNK
    assert H2 == P and chunk_columns == CHUNK * W and n_chunks * CHUNK == N_PAIRS
    assert N_ROUNDS * ROUND == N_PAIRS and PAIRS <= LOW_ROW

    with ExitStack() as ctx:
        def sb(name, shape, dt=F32):
            return ctx.enter_context(nc.sbuf_tensor(name, shape, dt))

        def psum(name, shape):
            return ctx.enter_context(nc.psum_tensor(name, shape, F32))

        def sem(name):
            return ctx.enter_context(nc.semaphore(name))

        w1_sb = sb("w1_sb", [P, 4, H1])
        bias_weights = sb("bias_weights", [P, H1])
        key_weights = sb("key_weights", [P, H1])
        w2_sb = sb("w2_sb", [P, HALVES, H2])
        w2_scaled = sb("w2_scaled", [P, HALVES, H2])
        w2_high = sb("w2_high", [P, HALVES, H2], F32R)
        w2_low = sb("w2_low", [P, HALVES, H2], F32R)
        w3_bc = sb("w3_bc", [P, H2])
        w3_bc_negative = sb("w3_bc_negative", [P, H2])
        w3_bc_size = sb("w3_bc_size", [P, H2])
        w3_col = sb("w3_col", [P, 1])
        w3_col_negative = sb("w3_col_negative", [P, 1])
        w3_col_size = sb("w3_col_size", [P, 1])
        w3_above = sb("w3_above", [P, 1])
        w3_below = sb("w3_below", [P, 1])
        b1_sb = sb("b1_sb", [P, HALVES])
        b2_sb = sb("b2_sb", [P, 1])
        b2_scaled = sb("b2_scaled", [P, 1])
        b3_sb = sb("b3_sb", [P, 1])
        sign_window = sb("sign_window", [P, PAIRS + P], F32R)
        selector_f = sb("selector_f", [P, PAIRS, P])
        selector = sb("selector", [P, PAIRS, P], F32R)
        per_user = sb("per_user", [P, N_GROUPS, 1 + HALVES, GROUP_USERS])

        keys = sb("keys", [P, ROUND, W])
        user_cols = sb("user_cols", [P, GROUPS_PER_ROUND, 1 + HALVES, GROUP_USERS])
        user_weights = sb("user_weights", [P, WEIGHT_BUFS, 2, H1])
        hidden1 = sb("hidden1", [P, HIDDEN1_BUFS, HALVES, W])
        hidden1_high = sb("hidden1_high", [P, HIDDEN1_BUFS, HALVES, W], F32R)
        hidden1_low = sb("hidden1_low", [P, HIDDEN1_BUFS, HALVES, W], F32R)
        hidden2 = sb("hidden2", [P, HIDDEN2_BUFS, W])
        hidden2_high = sb("hidden2_high", [P, HIDDEN2_BUFS, W], F32R)
        hidden2_low = sb("hidden2_low", [P, HIDDEN2_BUFS, W], F32R)
        mask_int = sb("mask_int", [P, GROUPS_PER_ROUND, W], I32)
        keep = sb("keep", [P, GROUPS_PER_ROUND, W])
        fill = sb("fill", [P, GROUPS_PER_ROUND, W])
        kept_scores = sb("kept_scores", [P, W])
        masked_scores = sb("masked_scores", [P, 2, N_KEYS])
        exps = sb("exps", [P, 2, N_KEYS])
        kept_exps = sb("kept_exps", [P, 2, N_KEYS])
        top = sb("top", [P, 2])
        minus_top = sb("minus_top", [P, 2])
        exp_sum = sb("exp_sum", [P, 2])
        kept_sum = sb("kept_sum", [P, 2])
        denominator = sb("denominator", [P, 2])
        inverse = sb("inverse", [P, 2])
        probs = sb("probs", [P, GROUPS_PER_ROUND, W], F32R)
        product = sb("product", [P, 2, 2, N_KEYS])
        pooled = sb("pooled", [P, GROUPS_PER_ROUND, GROUP_USERS])

        layer1_ps = psum("layer1_ps", [P, 2, HALVES, 512])
        layer2_ps = psum("layer2_ps", [P, 2, 512])
        score_ps = psum("score_ps", [P, 512])
        spread_ps = psum("spread_ps", [P, 512])

        consts_loaded = sem("consts_loaded")
        keys_loaded = [sem(f"keys_loaded{c}") for c in range(CHUNKS_PER_ROUND)]
        users_loaded = [sem(f"users_loaded{g}") for g in range(GROUPS_PER_ROUND)]
        mask_loaded = [sem(f"mask_loaded{g}") for g in range(GROUPS_PER_ROUND)]
        out_stored = [sem(f"out_stored{g}") for g in range(GROUPS_PER_ROUND)]
        setup_step = sem("setup_step")
        first_weights_ready = sem("first_weights_ready")
        bias_product_done = sem("bias_product_done")
        bias_done = sem("bias_done")
        masks_cleared = sem("masks_cleared")
        selector_step = sem("selector_step")
        selector_ready = sem("selector_ready")
        consts_ready = sem("consts_ready")
        weights_ready = sem("weights_ready")
        layer1_done = sem("layer1_done")
        hidden1_done = sem("hidden1_done")
        high1_done = sem("high1_done")
        low1_done = sem("low1_done")
        layer2_done = sem("layer2_done")
        hidden2_done = sem("hidden2_done")
        low2_done = sem("low2_done")
        scores_done = sem("scores_done")
        spread_done = sem("spread_done")
        pooled_done = sem("pooled_done")
        keep_done = sem("keep_done")
        fill_done = sem("fill_done")
        scores_read = sem("scores_read")
        masked_done = sem("masked_done")
        top_step = sem("top_step")
        exps_done = sem("exps_done")
        probs_step = sem("probs_step")
        probs_done = sem("probs_done")

        block = ctx.enter_context(nc.Block())

        def wait(eng, semaphore, value):
            if not isinstance(value, int) or value > 0:
                eng.wait_ge(semaphore, value)

        def rounds(eng, body, lag_in_tail):
            body(0, ROUND, lambda t, lag: t >= lag)
            with eng.Fori(1, N_ROUNDS) as r:
                body(r, ROUND, lambda t, lag: True)
            if lag_in_tail:
                body(N_ROUNDS, lag_in_tail, lambda t, lag: t < lag)

        def slot(t, lag, n):
            return (t - lag) % n

        @block.sync
        def _(sp):
            def load_users(group, g):
                sp.dma_start(user_cols[:, g], per_user[:, bass.ds(group, 1)].rearrange("p o a b -> p (o a) b")
                             ).then_inc(users_loaded[g], 16)

            def load_mask(group, g):
                for row in (0, LOW_ROW):
                    sp.dma_start(mask_int[row:row + PAIRS, g], mask[bass.ds(group * PAIRS, PAIRS), :]
                                 ).then_inc(mask_loaded[g], 16)

            def load_keys(chunk, c):
                sp.dma_start(keys[:, c * CHUNK:(c + 1) * CHUNK].rearrange("p a b -> p (a b)"),
                             keys_t[bass.ds(chunk, 1)].rearrange("o p n -> (o p) n")).then_inc(keys_loaded[c], 16)

            def store(group, g):
                sp.dma_start(out[bass.ds(group, 1)].rearrange("o p n -> (o p) n"), pooled[:, g]
                             ).then_inc(out_stored[g], 16)

            sp.dma_start(w1_sb[:], w1.rearrange("(a p) h -> p a h", p=P)).then_inc(consts_loaded, 16)
            sp.dma_start(per_user[:, :, 0, :], query_t.rearrange("p (g u) -> p g u", u=GROUP_USERS)
                         ).then_inc(consts_loaded, 16)
            sp.dma_start(b1_sb[:], b1).then_inc(consts_loaded, 16)
            sp.dma_start(w2_sb[:], w2.rearrange("(a p) h -> p a h", p=P)).then_inc(consts_loaded, 16)
            sp.dma_start(w3_bc[:], w3_row.to_broadcast([P, H2])).then_inc(consts_loaded, 16)
            sp.dma_start(w3_col[:], w3_column).then_inc(consts_loaded, 16)
            sp.dma_start(b2_sb[:], b2).then_inc(consts_loaded, 16)
            sp.dma_start(b3_sb[:], b3.to_broadcast([P, 1])).then_inc(consts_loaded, 16)
            load_keys(0, 0)
            sp.wait_ge(bias_done, 2 * HALVES)
            sp.wait_ge(masks_cleared, 1)
            for g in range(GROUPS_PER_ROUND):
                load_users(g, g)
                load_mask(g, g)
                for c in range(g * CHUNKS_PER_GROUP, (g + 1) * CHUNKS_PER_GROUP):
                    if c:
                        load_keys(c, c)
            with sp.Fori(1, N_ROUNDS) as r:
                for g in range(GROUPS_PER_ROUND):
                    group = r * GROUPS_PER_ROUND + g
                    before = group - GROUPS_PER_ROUND
                    sp.wait_ge(hidden1_done, (before + 1) * PAIRS)
                    sp.wait_ge(weights_ready, (before + 1) * PAIRS)
                    load_users(group, g)
                    sp.wait_ge(keep_done, before + 1)
                    load_mask(group, g)
                    for n in range(CHUNKS_PER_GROUP):
                        c = g * CHUNKS_PER_GROUP + n
                        sp.wait_ge(pooled_done, before * PAIRS + (n + 1) * CHUNK)
                        load_keys(r * CHUNKS_PER_ROUND + c, c)
                    store(before, g)
            for g in range(GROUPS_PER_ROUND):
                group = N_GROUPS - GROUPS_PER_ROUND + g
                sp.wait_ge(pooled_done, (group + 1) * PAIRS)
                store(group, g)
            for g in range(GROUPS_PER_ROUND):
                sp.wait_ge(out_stored[g], 16 * N_ROUNDS)

        @block.gpsimd
        def _(pool):
            nc.gpsimd.memset(mask_int[:], 0).then_inc(masks_cleared, 1)
            nc.gpsimd.memset(selector_f[:], 0.0).then_inc(selector_step, 1)
            pool.wait_ge(selector_step, 1)
            nc.gpsimd.affine_select(out=selector_f[:], in_=selector_f[:], compare_op=ALU.not_equal, fill=1.0,
                                    base=0, pattern=[[-1, PAIRS], [0, P]], channel_multiplier=1
                                    ).then_inc(selector_step, 1)
            pool.wait_ge(selector_step, 2)
            nc.gpsimd.affine_select(out=selector_f[:], in_=selector_f[:], compare_op=ALU.not_equal, fill=1.0,
                                    base=-LOW_ROW, pattern=[[-1, PAIRS], [0, P]], channel_multiplier=1
                                    ).then_inc(selector_ready, 1)

            def body(r, steps, active):
                first = r * ROUND
                for t in range(steps):
                    if active(t, LAG_HIDDEN1):
                        low1(first + (t - LAG_HIDDEN1), t)

            def low1(pair, t):
                b = (t - LAG_HIDDEN1) % HIDDEN1_BUFS
                pool.wait_ge(high1_done, pair + 1)
                wait(pool, layer2_done, pair - HIDDEN1_BUFS + 1)
                nc.gpsimd.tensor_tensor(hidden1_low[:, b], hidden1[:, b], hidden1_high[:, b].bitcast(F32),
                                        ALU.subtract).then_inc(low1_done, 1)

            rounds(pool, body, LAG_HIDDEN1)

        @block.scalar
        def _(act):
            act.wait_ge(consts_loaded, 16 * 8)
            for n in range(2):
                for h in range(HALVES):
                    act.wait_ge(bias_product_done, n * HALVES + h + 1)
                    nc.scalar.activation(
                        per_user[:, n * N_GROUPS // 2:(n + 1) * N_GROUPS // 2, 1 + h, :],
                        layer1_ps[:, n, h, :].rearrange("p (g u) -> p g u", u=GROUP_USERS),
                        ACT.Identity, bias=b1_sb[:, h:h + 1]).then_inc(bias_done, 1)
            act.wait_ge(consts_ready, 1)

            def hidden_layer1(pair, t, r):
                b, ps = (t - LAG_HIDDEN1) % HIDDEN1_BUFS, slot(t, LAG_HIDDEN1, 2)
                in_round = (t - LAG_HIDDEN1) % ROUND
                g, at = in_round // PAIRS, in_round % PAIRS
                if at == 0:
                    wait(act, users_loaded[g], (r + (1 if t >= LAG_HIDDEN1 else 0)) * 16)
                act.wait_ge(layer1_done, pair + 1)
                wait(act, low1_done, pair - HIDDEN1_BUFS + 1)
                for h in range(HALVES):
                    for s in range(2):
                        user = 2 * at + s
                        last = nc.scalar.activation(
                            hidden1[:, b, h, s * N_KEYS:(s + 1) * N_KEYS],
                            layer1_ps[:, ps, h, s * N_KEYS:(s + 1) * N_KEYS],
                            ACT.Relu, bias=user_cols[:, g, 1 + h, user:user + 1])
                last.then_inc(hidden1_done, 1)

            def hidden_layer2(pair, t):
                b, ps = (t - LAG_HIDDEN2) % HIDDEN2_BUFS, slot(t, LAG_HIDDEN2, 2)
                act.wait_ge(layer2_done, pair + 1)
                wait(act, scores_done, pair - HIDDEN2_BUFS + 1)
                nc.scalar.activation(hidden2[:, b], layer2_ps[:, ps, 0:W], ACT.Relu, bias=b2_scaled[:, 0:1])
                nc.scalar.activation(hidden2_high[:, b], layer2_ps[:, ps, 0:W], ACT.Relu,
                                     bias=b2_scaled[:, 0:1]).then_inc(hidden2_done, 1)

            def exponentials(group):
                act.wait_ge(top_step, group * 2 + 2)
                wait(act, probs_done, group)
                for s in range(2):
                    last = nc.scalar.activation(exps[:, s], masked_scores[:, s], ACT.Exp,
                                                bias=minus_top[:, s:s + 1], accum_out=exp_sum[:, s:s + 1])
                last.then_inc(exps_done, 1)

            def body(r, steps, active):
                first = r * ROUND
                for t in range(steps):
                    if active(t, LAG_HIDDEN1):
                        hidden_layer1(first + (t - LAG_HIDDEN1), t, r)
                    if active(t, LAG_HIDDEN2):
                        hidden_layer2(first + (t - LAG_HIDDEN2), t)
                    if (t - LAG_SOFTMAX) % PAIRS == 0 and active(t, LAG_SOFTMAX):
                        exponentials(r * GROUPS_PER_ROUND + (t - LAG_SOFTMAX) // PAIRS)

            rounds(act, body, LAG_SOFTMAX)

        @block.vector
        def _(dve):
            steps_done = [0]

            def then_wait(instruction):
                steps_done[0] += 1
                instruction.then_inc(setup_step, 1)
                dve.wait_ge(setup_step, steps_done[0])

            dve.wait_ge(consts_loaded, 16 * 8)
            nc.vector.tensor_tensor(bias_weights[:], w1_sb[:, 0], w1_sb[:, 2], ALU.add
                                    ).then_inc(first_weights_ready, 1)
            nc.vector.tensor_tensor(key_weights[:], w1_sb[:, 1], w1_sb[:, 2], ALU.subtract)
            nc.vector.tensor_scalar(w3_bc_negative[:], w3_bc[:], -1.0, None, ALU.mult)
            nc.vector.tensor_scalar(w3_above[:], w3_col[:], 0.0, None, ALU.is_gt)
            nc.vector.tensor_scalar(w3_below[:], w3_col[:], 0.0, None, ALU.is_lt)
            nc.vector.memset(sign_window[:].bitcast(mybir.dt.uint32), 0)
            then_wait(nc.vector.tensor_scalar(w3_col_negative[:], w3_col[:], -1.0, None, ALU.mult))
            nc.vector.tensor_tensor(w3_bc_size[:], w3_bc[:], w3_bc_negative[:], ALU.max)
            nc.vector.tensor_tensor(sign_window[:, PAIRS:PAIRS + 1], w3_above[:], w3_below[:], ALU.subtract)
            nc.vector.tensor_tensor(sign_window[:, PAIRS + LOW_ROW:PAIRS + LOW_ROW + 1], w3_above[:], w3_below[:],
                                    ALU.subtract)
            then_wait(nc.vector.tensor_tensor(w3_col_size[:], w3_col[:], w3_col_negative[:], ALU.max))
            nc.vector.tensor_tensor(b2_scaled[:], b2_sb[:], w3_col_size[:], ALU.mult)
            for h in range(HALVES):
                last = nc.vector.tensor_tensor(w2_scaled[:, h], w2_sb[:, h], w3_bc_size[:], ALU.mult)
            then_wait(last)
            then_wait(nc.vector.tensor_copy(w2_high[:], w2_scaled[:]))
            nc.vector.tensor_tensor(w2_low[:], w2_scaled[:], w2_high[:].bitcast(F32), ALU.subtract)
            dve.wait_ge(selector_ready, 1)
            nc.vector.tensor_copy(selector[:], selector_f[:]).then_inc(consts_ready, 1)
            dve.wait_ge(consts_ready, 1)

            def weights(pair, t, r):
                b = t % WEIGHT_BUFS
                g, at = t // PAIRS, t % PAIRS
                if at == 0:
                    wait(dve, users_loaded[g], r * 16 + 16)
                wait(dve, layer1_done, pair - WEIGHT_BUFS + 1)
                for s in range(2):
                    user = 2 * at + s
                    last = nc.vector.scalar_tensor_tensor(
                        out=user_weights[:, b, s], in0=w1_sb[:, 3], scalar=user_cols[:, g, 0, user:user + 1],
                        in1=key_weights[:], op0=ALU.mult, op1=ALU.add)
                last.then_inc(weights_ready, 1)

            def high1(pair, t):
                b = (t - LAG_HIDDEN1) % HIDDEN1_BUFS
                dve.wait_ge(hidden1_done, pair + 1)
                wait(dve, layer2_done, pair - HIDDEN1_BUFS + 1)
                nc.vector.tensor_copy(hidden1_high[:, b], hidden1[:, b]).then_inc(high1_done, 1)

            def low2(pair, t):
                b = (t - LAG_HIDDEN2_LOW) % HIDDEN2_BUFS
                dve.wait_ge(hidden2_done, pair + 1)
                wait(dve, scores_done, pair - HIDDEN2_BUFS + 1)
                nc.vector.tensor_tensor(hidden2_low[:, b], hidden2[:, b], hidden2_high[:, b].bitcast(F32),
                                        ALU.subtract).then_inc(low2_done, 1)

            def convert_mask(r, g):
                group = r * GROUPS_PER_ROUND + g
                wait(dve, mask_loaded[g], r * 32 + 32)
                nc.vector.tensor_scalar(keep[:, g], mask_int[:, g], 0.0, None, ALU.is_gt).then_inc(keep_done, 1)
                dve.wait_ge(keep_done, group + 1)
                nc.vector.tensor_scalar(fill[:, g], keep[:, g], -1.0, -MASKED_SCORE, ALU.add, ALU.mult
                                        ).then_inc(fill_done, 1)

            def softmax_top(group, g):
                dve.wait_ge(scores_done, (group + 1) * PAIRS)
                nc.vector.scalar_tensor_tensor(out=kept_scores[:], in0=score_ps[:, 0:W], scalar=b3_sb[:, 0:1],
                                               in1=keep[:, g], op0=ALU.add, op1=ALU.mult).then_inc(scores_read, 1)
                dve.wait_ge(scores_read, group + 1)
                dve.wait_ge(fill_done, group + 1)
                nc.vector.tensor_tensor(masked_scores[:].rearrange("p s n -> p (s n)"), kept_scores[:], fill[:, g],
                                        ALU.add).then_inc(masked_done, 1)
                dve.wait_ge(masked_done, group + 1)
                nc.vector.tensor_reduce(top[:], masked_scores[:], AX_X, ALU.max).then_inc(top_step, 1)
                dve.wait_ge(top_step, group * 2 + 1)
                nc.vector.tensor_scalar(minus_top[:], top[:], -1.0, None, ALU.mult).then_inc(top_step, 1)

            def softmax_probs(group, g):
                dve.wait_ge(exps_done, group + 1)
                for s in range(2):
                    last = nc.vector.scalar_tensor_tensor(
                        out=kept_exps[:, s], in0=exps[:, s], scalar=1.0, in1=keep[:, g, s * N_KEYS:(s + 1) * N_KEYS],
                        op0=ALU.mult, op1=ALU.mult, accum_out=kept_sum[:, s:s + 1])
                last.then_inc(probs_step, 1)
                dve.wait_ge(probs_step, group * 4 + 1)
                nc.vector.scalar_tensor_tensor(out=denominator[:], in0=exp_sum[:], scalar=LEAST_DENOMINATOR,
                                               in1=kept_sum[:], op0=ALU.mult, op1=ALU.max).then_inc(probs_step, 1)
                dve.wait_ge(probs_step, group * 4 + 2)
                nc.vector.reciprocal(inverse[:], denominator[:]).then_inc(probs_step, 1)
                dve.wait_ge(probs_step, group * 4 + 3)
                wait(dve, spread_done, (group - GROUPS_PER_ROUND + 1) * PAIRS)
                for s in range(2):
                    last = nc.vector.tensor_scalar(probs[:, g, s * N_KEYS:(s + 1) * N_KEYS], kept_exps[:, s],
                                                   inverse[:, s:s + 1], None, ALU.mult)
                last.then_inc(probs_step, 1)
                dve.wait_ge(probs_step, group * 4 + 4)
                for s in range(2):
                    low = probs[LOW_ROW:P, g, s * N_KEYS:(s + 1) * N_KEYS]
                    last = nc.vector.scalar_tensor_tensor(
                        out=low, in0=kept_exps[LOW_ROW:P, s], scalar=inverse[LOW_ROW:P, s:s + 1],
                        in1=low.bitcast(F32), op0=ALU.mult, op1=ALU.subtract)
                last.then_inc(probs_done, 1)

            def pool_keys(pair, t, r):
                in_round = (t - LAG_SPREAD) % ROUND
                g, at = in_round // PAIRS, in_round % PAIRS
                if at == 0:
                    wait(dve, out_stored[g], (r + (0 if t >= LAG_SPREAD else -1)) * 16)
                dve.wait_ge(spread_done, pair + 1)
                wait(dve, pooled_done, pair - 1)
                for s in range(2):
                    user = 2 * at + s
                    last = nc.vector.scalar_tensor_tensor(
                        out=product[:, at % 2, s], in0=keys[:, in_round, s * N_KEYS:(s + 1) * N_KEYS], scalar=1.0,
                        in1=spread_ps[:, s * N_KEYS:(s + 1) * N_KEYS], op0=ALU.mult, op1=ALU.mult,
                        accum_out=pooled[:, g, user:user + 1])
                last.then_inc(pooled_done, 1)

            def body(r, steps, active):
                first = r * ROUND
                for t in range(steps):
                    group = r * GROUPS_PER_ROUND + (t - LAG_SOFTMAX) // PAIRS
                    g = ((t - LAG_SOFTMAX) // PAIRS) % GROUPS_PER_ROUND
                    if (t - LAG_SOFTMAX) % PAIRS == 0 and active(t, LAG_SOFTMAX):
                        softmax_top(group, g)
                    if active(t, 0):
                        weights(first + t, t, r)
                        if t % PAIRS == PAIRS // 2:
                            convert_mask(r, t // PAIRS)
                    if active(t, LAG_SPREAD):
                        pool_keys(first + (t - LAG_SPREAD), t, r)
                    if active(t, LAG_HIDDEN1):
                        high1(first + (t - LAG_HIDDEN1), t)
                    if active(t, LAG_HIDDEN2_LOW):
                        low2(first + (t - LAG_HIDDEN2_LOW), t)
                    if (t - LAG_SOFTMAX) % PAIRS == 1 and active(t - 1, LAG_SOFTMAX):
                        softmax_probs(group, g)

            rounds(dve, body, LAG_SPREAD)

        @block.tensor
        def _(pe):
            pe.wait_ge(first_weights_ready, 1)
            for n in range(2):
                for h in range(HALVES):
                    nc.tensor.matmul(layer1_ps[:, n, h, :], bias_weights[:, h * P:(h + 1) * P],
                                     per_user[:, n * N_GROUPS // 2:(n + 1) * N_GROUPS // 2, 0, :],
                                     start=True, stop=True).then_inc(bias_product_done, 1)
            pe.wait_ge(bias_done, 2 * HALVES)

            def layer1(pair, t, r):
                b, ps = (t - LAG_LAYER1) % WEIGHT_BUFS, slot(t, LAG_LAYER1, 2)
                in_round = (t - LAG_LAYER1) % ROUND
                if in_round % CHUNK == 0:
                    wait(pe, keys_loaded[in_round // CHUNK], (r + (1 if t >= LAG_LAYER1 else 0)) * 16)
                pe.wait_ge(weights_ready, pair + 1)
                wait(pe, hidden1_done, pair - 1)
                for h in range(HALVES):
                    for s in range(2):
                        last = nc.tensor.matmul(layer1_ps[:, ps, h, s * N_KEYS:(s + 1) * N_KEYS],
                                                user_weights[:, b, s, h * P:(h + 1) * P],
                                                keys[:, in_round, s * N_KEYS:(s + 1) * N_KEYS],
                                                start=True, stop=True)
                last.then_inc(layer1_done, 1)

            def layer2(pair, t):
                b, ps = (t - LAG_LAYER2) % HIDDEN1_BUFS, slot(t, LAG_LAYER2, 2)
                parts = [(w, x, h) for h in range(HALVES) for w, x in
                         ((w2_high, hidden1_high), (w2_low, hidden1_high), (w2_high, hidden1_low))]
                pe.wait_ge(low1_done, pair + 1)
                wait(pe, hidden2_done, pair - 1)
                for n, (w, x, h) in enumerate(parts):
                    last = nc.tensor.matmul(layer2_ps[:, ps, 0:W], w[:, h], x[:, b, h],
                                            start=(n == 0), stop=(n == len(parts) - 1))
                last.then_inc(layer2_done, 1)

            def score(pair, t, r):
                b = (t - LAG_SCORE) % HIDDEN2_BUFS
                at = (t - LAG_SCORE) % PAIRS
                if at == 0:
                    wait(pe, scores_read, r * GROUPS_PER_ROUND + (t - LAG_SCORE) // PAIRS)
                pe.wait_ge(low2_done, pair + 1)
                signs = sign_window[:, PAIRS - at:PAIRS - at + P]
                nc.tensor.matmul(score_ps[:, 0:W], signs, hidden2_high[:, b], start=(at == 0), stop=False)
                nc.tensor.matmul(score_ps[:, 0:W], signs, hidden2_low[:, b], start=False,
                                 stop=(at == PAIRS - 1)).then_inc(scores_done, 1)

            def spread(pair, t, r):
                in_round = (t - LAG_SPREAD) % ROUND
                g, at = in_round // PAIRS, in_round % PAIRS
                if at == 0:
                    pe.wait_ge(probs_done, r * GROUPS_PER_ROUND + (t - LAG_SPREAD) // PAIRS + 1)
                wait(pe, pooled_done, pair)
                nc.tensor.matmul(spread_ps[:, 0:W], selector[:, at], probs[:, g], start=True, stop=True
                                 ).then_inc(spread_done, 1)

            pe.wait_ge(consts_ready, 1)

            def body(r, steps, active):
                first = r * ROUND
                for t in range(steps):
                    if active(t, LAG_LAYER1):
                        layer1(first + (t - LAG_LAYER1), t, r)
                    if active(t, LAG_LAYER2):
                        layer2(first + (t - LAG_LAYER2), t)
                    if active(t, LAG_SCORE):
                        score(first + (t - LAG_SCORE), t, r)
                    if active(t, LAG_SPREAD):
                        spread(first + (t - LAG_SPREAD), t, r)

            rounds(pe, body, LAG_SPREAD)



def kernel(r_query, r_keys, r_mask, L0_rec_W1, L0_rec_b1, L0_rec_W2, L0_rec_b2, L0_rec_W3, L0_rec_b3):
    import numpy as np
    import concourse.bacc as bacc
    from concourse.bass_utils import run_bass_kernel_spmd

    keys = np.asarray(r_keys)
    n_users, n_keys, d = keys.shape
    chunk_users = 2 * CHUNK
    group_users = 2 * PAIRS
    keys_t = keys.reshape(n_users // chunk_users, chunk_users, n_keys, d).transpose(0, 3, 1, 2)
    arrays = {
        "keys_t": keys_t.reshape(n_users // chunk_users, d, chunk_users * n_keys),
        "query_t": np.asarray(r_query).T,
        "mask": np.asarray(r_mask).reshape(n_users // 2, 2 * n_keys),
        "w1": np.asarray(L0_rec_W1),
        "b1": np.asarray(L0_rec_b1).reshape(-1, P).T,
        "w2": np.asarray(L0_rec_W2),
        "b2": np.asarray(L0_rec_b2).reshape(P, 1),
        "w3_column": np.asarray(L0_rec_W3).reshape(P, 1),
        "w3_row": np.asarray(L0_rec_W3).reshape(1, P),
        "b3": np.asarray(L0_rec_b3).reshape(1, 1),
    }
    arrays = {name: np.ascontiguousarray(a) for name, a in arrays.items()}
    nc = bacc.Bacc("TRN2", target_bir_lowering=False, num_devices=1)
    args = [nc.dram_tensor(name, a.shape, mybir.dt.from_np(a.dtype), kind="ExternalInput").ap()
            for name, a in arrays.items()]
    out = nc.dram_tensor("out", (n_users // group_users, d, group_users), F32, kind="ExternalOutput").ap()
    target_attention_kernel(nc, *args, out)
    got = run_bass_kernel_spmd(nc, [arrays], core_ids=[0]).results[0]["out"]
    return np.ascontiguousarray(np.asarray(got).transpose(0, 2, 1)).reshape(n_users, d)
```

```python
from contextlib import ExitStack

import concourse.bass as bass
from concourse import mybir

F32 = mybir.dt.float32
F32R = mybir.dt.float32r
I32 = mybir.dt.int32
ALU = mybir.AluOpType
ACT = mybir.ActivationFunctionType
AX_X = mybir.AxisListType.X

P = 128
MASKED_SCORE = -10000.0
LEAST_DENOMINATOR = 1e-12

PAIRS = 16
GROUPS_PER_ROUND = 2
ROUND = PAIRS * GROUPS_PER_ROUND
CHUNK = 2
TILE = 32
TILES = P // TILE
ROWS = PAIRS // TILES

LAG_LAYER1 = 2
LAG_HIDDEN1 = 2
LAG_SPLIT1 = 3
LAG_LAYER2 = 5
LAG_HIDDEN2 = 5
LAG_SCORE = 6
LAG_SCORES_READ = PAIRS + LAG_SCORE
LAG_TOP = LAG_SCORES_READ + 1
LAG_SUMS = LAG_SCORES_READ + 2
LAG_PROBS = LAG_SCORES_READ + 3
LAG_SPREAD = LAG_SCORES_READ + 4
LAG_POOL = LAG_SPREAD + 1

WEIGHT_BUFS = 4
HIDDEN1_BUFS = 4
HIDDEN2_BUFS = 8


def target_attention_kernel(nc, keys_t, query_t, mask, w1, b1, w2, b2, w3, b3, out):
    n_chunks, _, chunk_columns = keys_t.shape
    n_users = query_t.shape[1]
    N_KEYS = mask.shape[-1] // 2
    H1 = w1.shape[1]
    H2 = w2.shape[1]
    HALVES = H1 // P
    W = 2 * N_KEYS
    N_PAIRS = n_users // 2
    N_GROUPS = N_PAIRS // PAIRS
    GROUP_USERS = 2 * PAIRS
    N_ROUNDS = N_PAIRS // ROUND
    CHUNKS_PER_ROUND = ROUND // CHUNK
    CHUNKS_PER_GROUP = PAIRS // CHUNK
    assert H2 == P and chunk_columns == CHUNK * W and n_chunks * CHUNK == N_PAIRS
    assert N_ROUNDS * ROUND == N_PAIRS
    assert ROUND % HIDDEN1_BUFS == ROUND % HIDDEN2_BUFS == ROUND % WEIGHT_BUFS == PAIRS % TILES == 0
    assert 2 * ROWS <= TILE

    with ExitStack() as ctx:
        def sb(name, shape, dt=F32):
            return ctx.enter_context(nc.sbuf_tensor(name, shape, dt))

        def psum(name, shape):
            return ctx.enter_context(nc.psum_tensor(name, shape, F32))

        def sem(name):
            return ctx.enter_context(nc.semaphore(name))

        w1_sb = sb("w1_sb", [P, 4, H1])
        bias_weights = sb("bias_weights", [P, H1])
        w2_sb = sb("w2_sb", [P, HALVES, H2])
        w2_high = sb("w2_high", [P, HALVES, H2], F32R)
        w2_low = sb("w2_low", [P, HALVES, H2], F32R)
        b1_sb = sb("b1_sb", [P, HALVES])
        b2_sb = sb("b2_sb", [P, 1])
        b3_sb = sb("b3_sb", [P, 1])
        w3_window = sb("w3_window", [P, ROWS + TILE])
        selector_f = sb("selector_f", [P, ROWS, TILES, P])
        selector = sb("selector", [P, ROWS, TILES, P], F32R)
        low_table = sb("low_table", [P, TILES, ROWS])
        minus_low_row = sb("minus_low_row", [P, 1])
        all_queries = sb("all_queries", [P, n_users])
        all_biases = sb("all_biases", [P, N_GROUPS, HALVES, GROUP_USERS])

        keys = sb("keys", [P, ROUND, W])
        user_queries = sb("user_queries", [P, GROUPS_PER_ROUND, GROUP_USERS])
        user_biases = sb("user_biases", [P, GROUPS_PER_ROUND, HALVES, GROUP_USERS])
        user_weights = sb("user_weights", [P, WEIGHT_BUFS, 2, H1])
        hidden1 = sb("hidden1", [P, HIDDEN1_BUFS, HALVES, W])
        hidden1_high = sb("hidden1_high", [P, HIDDEN1_BUFS, HALVES, W], F32R)
        hidden1_low = sb("hidden1_low", [P, HIDDEN1_BUFS, HALVES, W], F32R)
        hidden2 = sb("hidden2", [P, HIDDEN2_BUFS, W])
        mask_int = sb("mask_int", [P, GROUPS_PER_ROUND, W], I32)
        keep = sb("keep", [P, GROUPS_PER_ROUND, W])
        fill = sb("fill", [P, GROUPS_PER_ROUND, W])
        kept_scores = sb("kept_scores", [P, W])
        masked_scores = sb("masked_scores", [P, 2, N_KEYS])
        exps = sb("exps", [P, 2, N_KEYS])
        kept_exps = sb("kept_exps", [P, 2, N_KEYS])
        top = sb("top", [P, 2])
        minus_top = sb("minus_top", [P, 2])
        exp_sum = sb("exp_sum", [P, 2])
        kept_sum = sb("kept_sum", [P, 2])
        denominator = sb("denominator", [P, 2])
        inverse = sb("inverse", [P, 2])
        values = sb("values", [P, 2, N_KEYS])
        values_high = sb("values_high", [P, W], F32R)
        probs = sb("probs", [P, GROUPS_PER_ROUND, W], F32R)
        product = sb("product", [P, 2, 2, N_KEYS])
        pooled = sb("pooled", [P, GROUPS_PER_ROUND, GROUP_USERS])

        layer1_ps = psum("layer1_ps", [P, 2, HALVES, 512])
        layer2_ps = psum("layer2_ps", [P, 512])
        score_ps = psum("score_ps", [P, 512])
        spread_ps = psum("spread_ps", [P, 512])
        key_weights = psum("key_weights", [P, 512])

        w1_loaded = sem("w1_loaded")
        queries_all_loaded = sem("queries_all_loaded")
        consts_loaded = sem("consts_loaded")
        w3_loaded = sem("w3_loaded")
        keys_loaded = [sem(f"keys_loaded{c}") for c in range(CHUNKS_PER_ROUND)]
        queries_loaded = [sem(f"queries_loaded{g}") for g in range(GROUPS_PER_ROUND)]
        biases_loaded = [sem(f"biases_loaded{g}") for g in range(GROUPS_PER_ROUND)]
        mask_loaded = [sem(f"mask_loaded{g}") for g in range(GROUPS_PER_ROUND)]
        out_stored = [sem(f"out_stored{g}") for g in range(GROUPS_PER_ROUND)]
        window_cleared = sem("window_cleared")
        first_weights_ready = sem("first_weights_ready")
        bias_product_done = sem("bias_product_done")
        bias_done = sem("bias_done")
        masks_cleared = sem("masks_cleared")
        selector_step = sem("selector_step")
        selector_ready = sem("selector_ready")
        w2_high_ready = sem("w2_high_ready")
        consts_ready = sem("consts_ready")
        weights_ready = sem("weights_ready")
        layer1_done = sem("layer1_done")
        hidden1_done = sem("hidden1_done")
        high1_done = sem("high1_done")
        low1_done = sem("low1_done")
        layer2_done = sem("layer2_done")
        hidden2_done = sem("hidden2_done")
        scores_done = sem("scores_done")
        spread_done = sem("spread_done")
        pooled_done = sem("pooled_done")
        keep_done = sem("keep_done")
        fill_done = sem("fill_done")
        scores_read = sem("scores_read")
        masked_done = sem("masked_done")
        top_step = sem("top_step")
        exps_done = sem("exps_done")
        sums_step = sem("sums_step")
        values_done = sem("values_done")
        high_probs_done = sem("high_probs_done")
        probs_done = sem("probs_done")

        block = ctx.enter_context(nc.Block())

        def wait(eng, semaphore, value):
            if not isinstance(value, int) or value > 0:
                eng.wait_ge(semaphore, value)

        def rounds(eng, body, lag_in_tail):
            body(0, ROUND, lambda t, lag: t >= lag)
            with eng.Fori(1, N_ROUNDS) as r:
                body(r, ROUND, lambda t, lag: True)
            if lag_in_tail:
                body(N_ROUNDS, lag_in_tail, lambda t, lag: t < lag)

        def starts_group(t, lag):
            return (t - lag) % PAIRS == 0

        def slot(t, lag, n):
            return (t - lag) % n

        def tile_and_row(at):
            return at % TILES, at // TILES

        def scored(r, t, lag, back=0):
            return r * (ROUND // TILES) + (t - lag - back) // TILES + 1

        BIAS_PARTS = 2
        bias_banks = [[layer1_ps[:, 1, h, :] for h in range(HALVES)], [score_ps[:], spread_ps[:]]]
        part_groups = N_GROUPS // BIAS_PARTS

        @block.sync
        def _(sp):
            def load_users(group, g):
                sp.dma_start(user_queries[:, g], all_queries[:, bass.ds(group * GROUP_USERS, GROUP_USERS)]
                             ).then_inc(queries_loaded[g], 16)
                sp.dma_start(user_biases[:, g], all_biases[:, bass.ds(group, 1)].rearrange("p o a b -> p (o a) b")
                             ).then_inc(biases_loaded[g], 16)

            def load_mask(group, g):
                for q in range(TILES):
                    sp.dma_start(mask_int[TILE * q:TILE * q + 2 * ROWS, g],
                                 mask[bass.ds(group, 1), q].rearrange("o p n -> (o p) n")
                                 ).then_inc(mask_loaded[g], 16)

            def load_keys(chunk, c):
                sp.dma_start(keys[:, c * CHUNK:(c + 1) * CHUNK].rearrange("p a b -> p (a b)"),
                             keys_t[bass.ds(chunk, 1)].rearrange("o p n -> (o p) n")).then_inc(keys_loaded[c], 16)

            def store(group, g):
                sp.dma_start(out[bass.ds(group, 1)].rearrange("o p n -> (o p) n"), pooled[:, g]
                             ).then_inc(out_stored[g], 16)

            sp.dma_start(w1_sb[:], w1.rearrange("(a p) h -> p a h", p=P)).then_inc(w1_loaded, 16)
            sp.dma_start(all_queries[:], query_t).then_inc(queries_all_loaded, 16)
            for c in range(CHUNKS_PER_GROUP):
                load_keys(c, c)
            sp.wait_ge(masks_cleared, 1)
            load_mask(0, 0)
            for c in range(CHUNKS_PER_GROUP, CHUNKS_PER_ROUND):
                load_keys(c, c)
            load_mask(1, 1)
            sp.wait_ge(bias_done, BIAS_PARTS * HALVES)
            for g in range(1, GROUPS_PER_ROUND):
                load_users(g, g)
            with sp.Fori(1, N_ROUNDS) as r:
                for g in range(GROUPS_PER_ROUND):
                    group = r * GROUPS_PER_ROUND + g
                    before = group - GROUPS_PER_ROUND
                    sp.wait_ge(hidden1_done, (before + 1) * PAIRS)
                    sp.wait_ge(weights_ready, (before + 1) * PAIRS)
                    load_users(group, g)
                    sp.wait_ge(keep_done, before + 1)
                    load_mask(group, g)
                    for n in range(CHUNKS_PER_GROUP):
                        c = g * CHUNKS_PER_GROUP + n
                        sp.wait_ge(pooled_done, before * PAIRS + (n + 1) * CHUNK)
                        load_keys(r * CHUNKS_PER_ROUND + c, c)
                    store(before, g)
            for g in range(GROUPS_PER_ROUND):
                group = N_GROUPS - GROUPS_PER_ROUND + g
                sp.wait_ge(pooled_done, (group + 1) * PAIRS)
                store(group, g)
            for g in range(GROUPS_PER_ROUND):
                sp.wait_ge(out_stored[g], 16 * N_ROUNDS)

        @block.gpsimd
        def _(pool):
            nc.gpsimd.memset(mask_int[:], 0).then_inc(masks_cleared, 1)
            nc.gpsimd.memset(selector_f[:], 0.0)
            nc.gpsimd.memset(low_table[:], 0.0).then_inc(selector_step, 1)
            pool.wait_ge(selector_step, 1)
            rows = [[-1, ROWS], [-TILE, TILES], [0, P]]
            nc.gpsimd.affine_select(out=low_table[:], in_=low_table[:], compare_op=ALU.not_equal, fill=-1.0,
                                    base=-ROWS, pattern=[[-TILE, TILES], [-1, ROWS]], channel_multiplier=1)
            nc.gpsimd.affine_select(out=selector_f[:], in_=selector_f[:], compare_op=ALU.not_equal, fill=1.0,
                                    base=0, pattern=rows, channel_multiplier=1).then_inc(selector_step, 1)
            pool.wait_ge(selector_step, 2)
            nc.gpsimd.affine_select(out=selector_f[:], in_=selector_f[:], compare_op=ALU.not_equal, fill=1.0,
                                    base=-ROWS, pattern=rows, channel_multiplier=1).then_inc(selector_ready, 1)

            def body(r, steps, active):
                first = r * ROUND
                for t in range(steps):
                    if active(t, LAG_SPLIT1):
                        low1(first + (t - LAG_SPLIT1), t)

            def low1(pair, t):
                b = (t - LAG_SPLIT1) % HIDDEN1_BUFS
                pool.wait_ge(high1_done, pair + 1)
                wait(pool, layer2_done, pair - HIDDEN1_BUFS + 1)
                nc.gpsimd.tensor_tensor(hidden1_low[:, b], hidden1[:, b], hidden1_high[:, b].bitcast(F32),
                                        ALU.subtract).then_inc(low1_done, 1)

            rounds(pool, body, LAG_SPLIT1)

        @block.scalar
        def _(act):
            for to, src in ((b1_sb[:], b1), (w2_sb[:], w2.rearrange("(a p) h -> p a h", p=P)), (b2_sb[:], b2),
                            (b3_sb[:], b3.to_broadcast([P, 1]))):
                act.dma_start(to, src).then_inc(consts_loaded, 16)
            act.wait_ge(window_cleared, 1)
            for column in (ROWS, 2 * ROWS):
                act.dma_start(w3_window[:, column:column + 1], w3).then_inc(w3_loaded, 16)
            act.wait_ge(consts_loaded, 16 * 4)
            for n in range(BIAS_PARTS):
                for h in range(HALVES):
                    act.wait_ge(bias_product_done, n * HALVES + h + 1)
                    nc.scalar.activation(
                        all_biases[:, n * part_groups:(n + 1) * part_groups, h, :],
                        bias_banks[n][h].rearrange("p (g u) -> p g u", u=GROUP_USERS),
                        ACT.Identity, bias=b1_sb[:, h:h + 1]).then_inc(bias_done, 1)
            act.wait_ge(bias_done, BIAS_PARTS * HALVES)

            def hidden_layer1(pair, t, r):
                b, ps = (t - LAG_HIDDEN1) % HIDDEN1_BUFS, slot(t, LAG_HIDDEN1, 2)
                in_round = (t - LAG_HIDDEN1) % ROUND
                g, at = in_round // PAIRS, in_round % PAIRS
                own_round = r if t >= LAG_HIDDEN1 else r - 1
                in_first = isinstance(own_round, int) and own_round == 0 and g == 0
                biases = all_biases[:, g] if in_first else user_biases[:, g]
                if at == 0 and not in_first:
                    act.wait_ge(biases_loaded[g], (own_round + min(g, 1)) * 16)
                act.wait_ge(layer1_done, pair + 1)
                wait(act, low1_done, pair - HIDDEN1_BUFS + 1)
                for h in range(HALVES):
                    for s in range(2):
                        user = 2 * at + s
                        last = nc.scalar.activation(
                            hidden1[:, b, h, s * N_KEYS:(s + 1) * N_KEYS],
                            layer1_ps[:, ps, h, s * N_KEYS:(s + 1) * N_KEYS],
                            ACT.Relu, bias=biases[:, h, user:user + 1])
                last.then_inc(hidden1_done, 1)

            def hidden_layer2(pair, t, r):
                b = slot(t, LAG_HIDDEN2, HIDDEN2_BUFS)
                act.wait_ge(layer2_done, pair + 1)
                wait(act, scores_done, scored(r, t, LAG_HIDDEN2, HIDDEN2_BUFS))
                nc.scalar.activation(hidden2[:, b], layer2_ps[:, 0:W], ACT.Relu, bias=b2_sb[:, 0:1]
                                     ).then_inc(hidden2_done, 1)

            def exponentials(group):
                act.wait_ge(top_step, group * 2 + 2)
                wait(act, sums_step, group * 3)
                for s in range(2):
                    last = nc.scalar.activation(exps[:, s], masked_scores[:, s], ACT.Exp,
                                                bias=minus_top[:, s:s + 1], accum_out=exp_sum[:, s:s + 1])
                last.then_inc(exps_done, 1)

            def make_values(group):
                act.wait_ge(sums_step, group * 3 + 3)
                wait(act, probs_done, group)
                for s in range(2):
                    last = nc.scalar.activation(values[:, s], kept_exps[:, s], ACT.Copy, scale=inverse[:, s:s + 1])
                last.then_inc(values_done, 1)

            def body(r, steps, active):
                first = r * ROUND
                for t in range(steps):
                    if active(t, LAG_HIDDEN1):
                        hidden_layer1(first + (t - LAG_HIDDEN1), t, r)
                    if active(t, LAG_HIDDEN2):
                        hidden_layer2(first + (t - LAG_HIDDEN2), t, r)
                    if starts_group(t, LAG_TOP) and active(t, LAG_TOP):
                        exponentials(r * GROUPS_PER_ROUND + (t - LAG_TOP) // PAIRS)
                    if starts_group(t, LAG_SUMS) and active(t, LAG_SUMS):
                        make_values(r * GROUPS_PER_ROUND + (t - LAG_SUMS) // PAIRS)

            rounds(act, body, LAG_SUMS + 1)

        @block.vector
        def _(dve):
            nc.vector.memset(w3_window[:], 0.0).then_inc(window_cleared, 1)
            dve.wait_ge(w1_loaded, 16)
            nc.vector.tensor_tensor(bias_weights[:], w1_sb[:, 0], w1_sb[:, 2], ALU.add)
            nc.vector.tensor_tensor(key_weights[:, 0:H1], w1_sb[:, 1], w1_sb[:, 2], ALU.subtract
                                    ).then_inc(first_weights_ready, 1)
            dve.wait_ge(queries_all_loaded, 16)
            dve.wait_ge(first_weights_ready, 1)

            def finish_constants():
                dve.wait_ge(consts_loaded, 16 * 4)
                nc.vector.tensor_copy(w2_high[:], w2_sb[:]).then_inc(w2_high_ready, 1)
                dve.wait_ge(w2_high_ready, 1)
                nc.vector.tensor_tensor(w2_low[:], w2_sb[:], w2_high[:].bitcast(F32), ALU.subtract)
                dve.wait_ge(selector_ready, 1)
                nc.vector.tensor_reduce(minus_low_row[:], low_table[:].rearrange("p q i -> p (q i)"), AX_X, ALU.add)
                nc.vector.tensor_copy(selector[:], selector_f[:]).then_inc(consts_ready, 1)

            def weights(pair, t, r):
                b = t % WEIGHT_BUFS
                g, at = t // PAIRS, t % PAIRS
                in_first = isinstance(r, int) and g == 0
                queries = all_queries[:, g * GROUP_USERS:(g + 1) * GROUP_USERS] if in_first else user_queries[:, g]
                if at == 0 and not in_first:
                    dve.wait_ge(queries_loaded[g], (r + min(g, 1)) * 16)
                wait(dve, layer1_done, pair - WEIGHT_BUFS + 1)
                for s in range(2):
                    user = 2 * at + s
                    last = nc.vector.scalar_tensor_tensor(
                        out=user_weights[:, b, s], in0=w1_sb[:, 3], scalar=queries[:, user:user + 1],
                        in1=key_weights[:, 0:H1], op0=ALU.mult, op1=ALU.add)
                last.then_inc(weights_ready, 1)

            def high1(pair, t):
                b = (t - LAG_SPLIT1) % HIDDEN1_BUFS
                dve.wait_ge(hidden1_done, pair + 1)
                wait(dve, layer2_done, pair - HIDDEN1_BUFS + 1)
                nc.vector.tensor_copy(hidden1_high[:, b], hidden1[:, b]).then_inc(high1_done, 1)

            def convert_mask(r, g):
                group = r * GROUPS_PER_ROUND + g
                wait(dve, mask_loaded[g], (r + 1) * 16 * TILES)
                nc.vector.tensor_scalar(keep[:, g], mask_int[:, g], 0.0, None, ALU.is_gt).then_inc(keep_done, 1)
                dve.wait_ge(keep_done, group + 1)
                nc.vector.tensor_scalar(fill[:, g], keep[:, g], -1.0, -MASKED_SCORE, ALU.add, ALU.mult
                                        ).then_inc(fill_done, 1)

            def read_scores(group, g):
                dve.wait_ge(scores_done, (group + 1) * ROWS)
                nc.vector.scalar_tensor_tensor(out=kept_scores[:], in0=score_ps[:, 0:W], scalar=b3_sb[:, 0:1],
                                               in1=keep[:, g], op0=ALU.add, op1=ALU.mult).then_inc(scores_read, 1)
                dve.wait_ge(scores_read, group + 1)
                dve.wait_ge(fill_done, group + 1)
                nc.vector.tensor_tensor(masked_scores[:].rearrange("p s n -> p (s n)"), kept_scores[:], fill[:, g],
                                        ALU.add).then_inc(masked_done, 1)

            def find_top(group, g):
                dve.wait_ge(masked_done, group + 1)
                nc.vector.tensor_reduce(top[:], masked_scores[:], AX_X, ALU.max).then_inc(top_step, 1)
                dve.wait_ge(top_step, group * 2 + 1)
                nc.vector.tensor_scalar(minus_top[:], top[:], -1.0, None, ALU.mult).then_inc(top_step, 1)

            def sums(group, g):
                dve.wait_ge(exps_done, group + 1)
                wait(dve, values_done, group)
                for s in range(2):
                    last = nc.vector.scalar_tensor_tensor(
                        out=kept_exps[:, s], in0=exps[:, s], scalar=1.0, in1=keep[:, g, s * N_KEYS:(s + 1) * N_KEYS],
                        op0=ALU.mult, op1=ALU.mult, accum_out=kept_sum[:, s:s + 1])
                last.then_inc(sums_step, 1)
                dve.wait_ge(sums_step, group * 3 + 1)
                nc.vector.scalar_tensor_tensor(out=denominator[:], in0=exp_sum[:], scalar=LEAST_DENOMINATOR,
                                               in1=kept_sum[:], op0=ALU.mult, op1=ALU.max).then_inc(sums_step, 1)
                dve.wait_ge(sums_step, group * 3 + 2)
                nc.vector.reciprocal(inverse[:], denominator[:]).then_inc(sums_step, 1)

            def make_probs(group, g):
                dve.wait_ge(values_done, group + 1)
                values_row = values[:].rearrange("p s n -> p (s n)")
                nc.vector.tensor_copy(values_high[:], values_row).then_inc(high_probs_done, 1)
                dve.wait_ge(high_probs_done, group + 1)
                wait(dve, spread_done, (group - GROUPS_PER_ROUND + 1) * PAIRS)
                nc.vector.scalar_tensor_tensor(out=probs[:, g], in0=values_high[:].bitcast(F32),
                                               scalar=minus_low_row[:, 0:1], in1=values_row,
                                               op0=ALU.mult, op1=ALU.add).then_inc(probs_done, 1)

            def pool_keys(pair, t, r):
                in_round = (t - LAG_POOL) % ROUND
                g, at = in_round // PAIRS, in_round % PAIRS
                if at == 0:
                    wait(dve, out_stored[g], (r + (0 if t >= LAG_POOL else -1)) * 16)
                dve.wait_ge(spread_done, pair + 1)
                wait(dve, pooled_done, pair - 1)
                for s in range(2):
                    user = 2 * at + s
                    last = nc.vector.scalar_tensor_tensor(
                        out=product[:, at % 2, s], in0=keys[:, in_round, s * N_KEYS:(s + 1) * N_KEYS], scalar=1.0,
                        in1=spread_ps[:, s * N_KEYS:(s + 1) * N_KEYS], op0=ALU.mult, op1=ALU.mult,
                        accum_out=pooled[:, g, user:user + 1])
                last.then_inc(pooled_done, 1)

            def body(r, steps, active):
                first = r * ROUND
                for t in range(steps):
                    for part, lag in ((read_scores, LAG_SCORES_READ), (find_top, LAG_TOP), (sums, LAG_SUMS),
                                      (make_probs, LAG_PROBS)):
                        if starts_group(t, lag) and active(t, lag):
                            groups = (t - lag) // PAIRS
                            part(r * GROUPS_PER_ROUND + groups, groups % GROUPS_PER_ROUND)
                    if active(t, LAG_POOL):
                        pool_keys(first + (t - LAG_POOL), t, r)
                    if active(t, LAG_SPLIT1):
                        high1(first + (t - LAG_SPLIT1), t)
                    if active(t, 0):
                        weights(first + t, t, r)
                        if t % PAIRS == PAIRS // 2:
                            convert_mask(r, t // PAIRS)
                        if t == 1 and isinstance(r, int):
                            finish_constants()

            rounds(dve, body, LAG_POOL)

        @block.tensor
        def _(pe):
            pe.wait_ge(first_weights_ready, 1)
            pe.wait_ge(queries_all_loaded, 16)
            part_users = n_users // BIAS_PARTS
            for n in range(BIAS_PARTS):
                for h in range(HALVES):
                    nc.tensor.matmul(bias_banks[n][h], bias_weights[:, h * P:(h + 1) * P],
                                     all_queries[:, n * part_users:(n + 1) * part_users],
                                     start=True, stop=True).then_inc(bias_product_done, 1)

            def layer1(pair, t, r):
                b, ps = (t - LAG_LAYER1) % WEIGHT_BUFS, slot(t, LAG_LAYER1, 2)
                in_round = (t - LAG_LAYER1) % ROUND
                if in_round % CHUNK == 0:
                    wait(pe, keys_loaded[in_round // CHUNK], (r + (1 if t >= LAG_LAYER1 else 0)) * 16)
                pe.wait_ge(weights_ready, pair + 1)
                wait(pe, hidden1_done, pair - 1)
                if isinstance(pair, int) and pair == 1:
                    pe.wait_ge(bias_done, BIAS_PARTS * HALVES)
                for h in range(HALVES):
                    for s in range(2):
                        last = nc.tensor.matmul(layer1_ps[:, ps, h, s * N_KEYS:(s + 1) * N_KEYS],
                                                user_weights[:, b, s, h * P:(h + 1) * P],
                                                keys[:, in_round, s * N_KEYS:(s + 1) * N_KEYS],
                                                start=True, stop=True)
                last.then_inc(layer1_done, 1)

            def layer2(pair, t):
                b = slot(t, LAG_LAYER2, HIDDEN1_BUFS)
                parts = [(w, x, h) for h in range(HALVES) for w, x in
                         ((w2_high, hidden1_high), (w2_low, hidden1_high), (w2_high, hidden1_low))]
                pe.wait_ge(low1_done, pair + 1)
                if isinstance(pair, int) and pair == 0:
                    pe.wait_ge(consts_ready, 1)
                wait(pe, hidden2_done, pair)
                for n, (w, x, h) in enumerate(parts):
                    last = nc.tensor.matmul(layer2_ps[:, 0:W], w[:, h], x[:, b, h],
                                            start=(n == 0), stop=(n == len(parts) - 1))
                last.then_inc(layer2_done, 1)

            def score(pair, t, r):
                row = (t - LAG_SCORE) % PAIRS // TILES
                if row == 0:
                    wait(pe, scores_read, r * GROUPS_PER_ROUND + (t - LAG_SCORE) // PAIRS)
                pe.wait_ge(hidden2_done, pair + 1)
                if isinstance(pair, int) and pair == TILES - 1:
                    pe.wait_ge(w3_loaded, 16 * 2)
                for q in range(TILES):
                    b = slot(t, LAG_SCORE + TILES - 1 - q, HIDDEN2_BUFS)
                    last = nc.tensor.matmul(score_ps[TILE * q:TILE * (q + 1), 0:W],
                                            w3_window[:, ROWS - row:ROWS - row + TILE], hidden2[:, b],
                                            start=(row == 0), stop=(row == ROWS - 1))
                last.then_inc(scores_done, 1)

            def spread(pair, t, r):
                in_round = (t - LAG_SPREAD) % ROUND
                g, at = in_round // PAIRS, in_round % PAIRS
                q, row = tile_and_row(at)
                if at == 0:
                    pe.wait_ge(probs_done, r * GROUPS_PER_ROUND + (t - LAG_SPREAD) // PAIRS + 1)
                wait(pe, pooled_done, pair)
                nc.tensor.matmul(spread_ps[:, 0:W], selector[:, row, q], probs[:, g], start=True, stop=True
                                 ).then_inc(spread_done, 1)

            def body(r, steps, active):
                first = r * ROUND
                for t in range(steps):
                    if active(t, LAG_LAYER1):
                        layer1(first + (t - LAG_LAYER1), t, r)
                    if active(t, LAG_LAYER2):
                        layer2(first + (t - LAG_LAYER2), t)
                    if active(t, LAG_SPREAD):
                        spread(first + (t - LAG_SPREAD), t, r)
                    if (t - LAG_SCORE) % TILES == TILES - 1 and active(t, LAG_SCORE):
                        score(first + (t - LAG_SCORE), t, r)

            rounds(pe, body, LAG_SPREAD)



def kernel(r_query, r_keys, r_mask, L0_rec_W1, L0_rec_b1, L0_rec_W2, L0_rec_b2, L0_rec_W3, L0_rec_b3):
    import numpy as np
    import concourse.bacc as bacc
    from concourse.bass_utils import run_bass_kernel_spmd

    keys = np.asarray(r_keys)
    n_users, n_keys, d = keys.shape
    chunk_users = 2 * CHUNK
    group_users = 2 * PAIRS
    keys_t = keys.reshape(n_users // chunk_users, chunk_users, n_keys, d).transpose(0, 3, 1, 2)
    masks = np.asarray(r_mask).reshape(n_users // group_users, ROWS, TILES, 2 * n_keys).transpose(0, 2, 1, 3)
    masks = np.concatenate([masks, masks], axis=2)
    arrays = {
        "keys_t": keys_t.reshape(n_users // chunk_users, d, chunk_users * n_keys),
        "query_t": np.asarray(r_query).T,
        "mask": masks,
        "w1": np.asarray(L0_rec_W1),
        "b1": np.asarray(L0_rec_b1).reshape(-1, P).T,
        "w2": np.asarray(L0_rec_W2),
        "b2": np.asarray(L0_rec_b2).reshape(P, 1),
        "w3": np.asarray(L0_rec_W3).reshape(P, 1),
        "b3": np.asarray(L0_rec_b3).reshape(1, 1),
    }
    arrays = {name: np.ascontiguousarray(a) for name, a in arrays.items()}
    nc = bacc.Bacc("TRN2", target_bir_lowering=False, num_devices=1)
    args = [nc.dram_tensor(name, a.shape, mybir.dt.from_np(a.dtype), kind="ExternalInput").ap()
            for name, a in arrays.items()]
    out = nc.dram_tensor("out", (n_users // group_users, d, group_users), F32, kind="ExternalOutput").ap()
    target_attention_kernel(nc, *args, out)
    got = run_bass_kernel_spmd(nc, [arrays], core_ids=[0]).results[0]["out"]
    return np.ascontiguousarray(np.asarray(got).transpose(0, 2, 1)).reshape(n_users, d)
```

```python
from contextlib import ExitStack

import concourse.bass as bass
from concourse import mybir

F32 = mybir.dt.float32
F32R = mybir.dt.float32r
I32 = mybir.dt.int32
ALU = mybir.AluOpType
ACT = mybir.ActivationFunctionType
AX_X = mybir.AxisListType.X

P = 128
MASKED_SCORE = -10000.0
LEAST_DENOMINATOR = 1e-12

PAIRS = 16
GROUPS_PER_ROUND = 2
ROUND = PAIRS * GROUPS_PER_ROUND
CHUNK = 2
TILE = 32
TILES = P // TILE
SCORED = 16
ROWS = PAIRS // TILES

LAG_LAYER1 = 2
LAG_HIDDEN1 = 2
LAG_SPLIT1 = 3
LAG_LAYER2 = 5
LAG_HIDDEN2 = 5
LAG_SCORE = 6
LAG_SCORES_READ = PAIRS + LAG_SCORE
LAG_TOP = LAG_SCORES_READ + 2
LAG_SUMS = LAG_SCORES_READ + 3
LAG_INVERSE = LAG_SCORES_READ + 4
LAG_VALUES = LAG_SCORES_READ + 4
LAG_PROBS = LAG_SCORES_READ + 5
LAG_SPREAD = LAG_SCORES_READ + 6
LAG_POOL = LAG_SPREAD + 1
MASK_STEP = PAIRS - 2

WEIGHT_BUFS = 4
HIDDEN1_BUFS = 4
HIDDEN2_BUFS = 32


def target_attention_kernel(nc, keys_t, query_t, mask, w1, b1, w2, b2, w3, b3, out):
    n_chunks, _, chunk_columns = keys_t.shape
    n_users = query_t.shape[1]
    N_KEYS = mask.shape[-1] // 2
    H1 = w1.shape[1]
    H2 = w2.shape[1]
    HALVES = H1 // P
    W = 2 * N_KEYS
    N_PAIRS = n_users // 2
    N_GROUPS = N_PAIRS // PAIRS
    GROUP_USERS = 2 * PAIRS
    N_ROUNDS = N_PAIRS // ROUND
    CHUNKS_PER_ROUND = ROUND // CHUNK
    CHUNKS_PER_GROUP = PAIRS // CHUNK
    assert H2 == P and chunk_columns == CHUNK * W and n_chunks * CHUNK == N_PAIRS
    assert N_ROUNDS * ROUND == N_PAIRS
    assert ROUND % HIDDEN1_BUFS == ROUND % HIDDEN2_BUFS == ROUND % WEIGHT_BUFS == PAIRS % TILES == 0
    assert 2 * ROWS <= TILE and SCORED % TILES == PAIRS % SCORED == HIDDEN2_BUFS % SCORED == 0

    with ExitStack() as ctx:
        def sb(name, shape, dt=F32):
            return ctx.enter_context(nc.sbuf_tensor(name, shape, dt))

        def psum(name, shape):
            return ctx.enter_context(nc.psum_tensor(name, shape, F32))

        def sem(name):
            return ctx.enter_context(nc.semaphore(name))

        w1_sb = sb("w1_sb", [P, 4, H1])
        bias_weights = sb("bias_weights", [P, H1])
        w2_sb = sb("w2_sb", [P, HALVES, H2])
        w2_high = sb("w2_high", [P, HALVES, H2], F32R)
        w2_low = sb("w2_low", [P, HALVES, H2], F32R)
        b1_sb = sb("b1_sb", [P, HALVES])
        b2_sb = sb("b2_sb", [P, 1])
        b3_sb = sb("b3_sb", [P, 1])
        w3_window = sb("w3_window", [P, ROWS + TILE])
        selector = sb("selector", [P, ROWS, TILES, P], F32R)
        low_table = sb("low_table", [P, TILES, ROWS])
        minus_low_row = sb("minus_low_row", [P, 1])
        all_queries = sb("all_queries", [P, n_users])
        all_biases = sb("all_biases", [P, N_GROUPS, HALVES, GROUP_USERS])

        keys = sb("keys", [P, ROUND, W])
        user_queries = sb("user_queries", [P, GROUPS_PER_ROUND, GROUP_USERS])
        user_biases = sb("user_biases", [P, GROUPS_PER_ROUND, HALVES, GROUP_USERS])
        user_weights = sb("user_weights", [P, WEIGHT_BUFS, 2, H1])
        hidden1 = sb("hidden1", [P, HIDDEN1_BUFS, HALVES, W])
        hidden1_high = sb("hidden1_high", [P, HIDDEN1_BUFS, HALVES, W], F32R)
        hidden1_low = sb("hidden1_low", [P, HIDDEN1_BUFS, HALVES, W], F32R)
        hidden2 = sb("hidden2", [P, HIDDEN2_BUFS, W])
        selector_f = hidden2[:].rearrange("p b n -> p (b n)")[:, 0:ROWS * TILES * P].rearrange(
            "p (i q m) -> p i q m", i=ROWS, q=TILES)
        mask_int = sb("mask_int", [P, GROUPS_PER_ROUND, W], I32)
        keep = sb("keep", [P, GROUPS_PER_ROUND, W])
        fill = sb("fill", [P, GROUPS_PER_ROUND, W])
        kept_scores = sb("kept_scores", [P, W])
        masked_scores = sb("masked_scores", [P, 2, N_KEYS])
        exps = sb("exps", [P, 2, N_KEYS])
        kept_exps = sb("kept_exps", [P, 2, N_KEYS])
        top = sb("top", [P, 2])
        minus_top = sb("minus_top", [P, 2])
        exp_sum = sb("exp_sum", [P, 2])
        kept_sum = sb("kept_sum", [P, 2])
        denominator = sb("denominator", [P, 2])
        inverse = sb("inverse", [P, 2])
        values = sb("values", [P, 2, N_KEYS])
        values_high = sb("values_high", [P, W], F32R)
        probs = sb("probs", [P, GROUPS_PER_ROUND, W], F32R)
        product = sb("product", [P, 2, 2, N_KEYS])
        pooled = sb("pooled", [P, GROUPS_PER_ROUND, GROUP_USERS])

        layer1_ps = psum("layer1_ps", [P, 2, HALVES, 512])
        layer2_ps = psum("layer2_ps", [P, 512])
        score_ps = psum("score_ps", [P, 512])
        spread_ps = psum("spread_ps", [P, 512])
        key_weights = psum("key_weights", [P, 512])

        w1_loaded = sem("w1_loaded")
        queries_all_loaded = sem("queries_all_loaded")
        consts_loaded = sem("consts_loaded")
        w3_loaded = sem("w3_loaded")
        keys_loaded = [sem(f"keys_loaded{c}") for c in range(CHUNKS_PER_ROUND)]
        queries_loaded = [sem(f"queries_loaded{g}") for g in range(GROUPS_PER_ROUND)]
        biases_loaded = [sem(f"biases_loaded{g}") for g in range(GROUPS_PER_ROUND)]
        mask_loaded = [sem(f"mask_loaded{g}") for g in range(GROUPS_PER_ROUND)]
        out_stored = [sem(f"out_stored{g}") for g in range(GROUPS_PER_ROUND)]
        window_cleared = sem("window_cleared")
        first_weights_ready = sem("first_weights_ready")
        bias_product_done = sem("bias_product_done")
        bias_done = sem("bias_done")
        masks_cleared = sem("masks_cleared")
        selector_step = sem("selector_step")
        selector_ready = sem("selector_ready")
        w2_high_ready = sem("w2_high_ready")
        consts_ready = sem("consts_ready")
        weights_ready = sem("weights_ready")
        layer1_done = sem("layer1_done")
        hidden1_done = sem("hidden1_done")
        high1_done = sem("high1_done")
        low1_done = sem("low1_done")
        layer2_done = sem("layer2_done")
        hidden2_done = sem("hidden2_done")
        scores_done = sem("scores_done")
        spread_done = sem("spread_done")
        pooled_done = sem("pooled_done")
        keep_done = sem("keep_done")
        fill_done = sem("fill_done")
        scores_read = sem("scores_read")
        masked_done = sem("masked_done")
        top_step = sem("top_step")
        exps_done = sem("exps_done")
        sums_step = sem("sums_step")
        values_done = sem("values_done")
        high_probs_done = sem("high_probs_done")
        probs_done = sem("probs_done")

        block = ctx.enter_context(nc.Block())

        def wait(eng, semaphore, value):
            if not isinstance(value, int) or value > 0:
                eng.wait_ge(semaphore, value)

        def rounds(eng, body, lag_in_tail):
            body(0, ROUND, lambda t, lag: t >= lag)
            with eng.Fori(1, N_ROUNDS) as r:
                body(r, ROUND, lambda t, lag: True)
            body(N_ROUNDS, lag_in_tail, lambda t, lag: t < lag)

        def starts_group(t, lag):
            return (t - lag) % PAIRS == 0

        def slot(t, lag, n):
            return (t - lag) % n

        def tile_and_row(at):
            return at % TILES, at // TILES

        def scored(r, t, lag, back=0):
            return r * (ROUND // SCORED) + (t - lag - back) // SCORED + 1

        def spread_bank(r, t, at):
            ahead = isinstance(r, int) and r == N_ROUNDS and t >= LAG_LAYER2
            return layer1_ps[:, at // 2 % 2, at % 2] if ahead else spread_ps

        BIAS_PARTS = 2
        bias_banks = [[layer1_ps[:, 1, h, :] for h in range(HALVES)], [score_ps[:], spread_ps[:]]]
        part_groups = N_GROUPS // BIAS_PARTS

        @block.sync
        def _(sp):
            def load_users(group, g):
                sp.dma_start(user_queries[:, g], all_queries[:, bass.ds(group * GROUP_USERS, GROUP_USERS)]
                             ).then_inc(queries_loaded[g], 16)
                sp.dma_start(user_biases[:, g], all_biases[:, bass.ds(group, 1)].rearrange("p o a b -> p (o a) b")
                             ).then_inc(biases_loaded[g], 16)

            def load_mask(group, g):
                for q in range(TILES):
                    sp.dma_start(mask_int[TILE * q:TILE * q + 2 * ROWS, g],
                                 mask[bass.ds(group, 1), q].rearrange("o p n -> (o p) n")
                                 ).then_inc(mask_loaded[g], 16)

            def load_keys(chunk, c):
                sp.dma_start(keys[:, c * CHUNK:(c + 1) * CHUNK].rearrange("p a b -> p (a b)"),
                             keys_t[bass.ds(chunk, 1)].rearrange("o p n -> (o p) n")).then_inc(keys_loaded[c], 16)

            def store(group, g):
                sp.dma_start(out[bass.ds(group, 1)].rearrange("o p n -> (o p) n"), pooled[:, g]
                             ).then_inc(out_stored[g], 16)

            sp.dma_start(w1_sb[:], w1.rearrange("(a p) h -> p a h", p=P)).then_inc(w1_loaded, 16)
            for c in range(CHUNKS_PER_GROUP):
                load_keys(c, c)
            sp.wait_ge(masks_cleared, 1)
            load_mask(0, 0)
            for c in range(CHUNKS_PER_GROUP, CHUNKS_PER_ROUND):
                load_keys(c, c)
            load_mask(1, 1)
            sp.wait_ge(bias_done, BIAS_PARTS * HALVES)
            for g in range(1, GROUPS_PER_ROUND):
                load_users(g, g)
            with sp.Fori(1, N_ROUNDS) as r:
                for g in range(GROUPS_PER_ROUND):
                    group = r * GROUPS_PER_ROUND + g
                    before = group - GROUPS_PER_ROUND
                    sp.wait_ge(hidden1_done, (before + 1) * PAIRS)
                    sp.wait_ge(weights_ready, (before + 1) * PAIRS)
                    load_users(group, g)
                    sp.wait_ge(keep_done, before + 1)
                    load_mask(group, g)
                    for n in range(CHUNKS_PER_GROUP):
                        c = g * CHUNKS_PER_GROUP + n
                        sp.wait_ge(pooled_done, before * PAIRS + (n + 1) * CHUNK)
                        load_keys(r * CHUNKS_PER_ROUND + c, c)
                    store(before, g)
            for g in range(GROUPS_PER_ROUND):
                group = N_GROUPS - GROUPS_PER_ROUND + g
                sp.wait_ge(pooled_done, (group + 1) * PAIRS)
                store(group, g)
            for g in range(GROUPS_PER_ROUND):
                sp.wait_ge(out_stored[g], 16 * N_ROUNDS)

        @block.gpsimd
        def _(pool):
            nc.gpsimd.memset(mask_int[:], 0).then_inc(masks_cleared, 1)
            nc.gpsimd.memset(selector_f, 0.0)
            nc.gpsimd.memset(low_table[:], 0.0).then_inc(selector_step, 1)
            pool.wait_ge(selector_step, 1)
            rows = [[-1, ROWS], [-TILE, TILES], [0, P]]
            nc.gpsimd.affine_select(out=low_table[:], in_=low_table[:], compare_op=ALU.not_equal, fill=-1.0,
                                    base=-ROWS, pattern=[[-TILE, TILES], [-1, ROWS]], channel_multiplier=1)
            nc.gpsimd.affine_select(out=selector_f, in_=selector_f, compare_op=ALU.not_equal, fill=1.0,
                                    base=0, pattern=rows, channel_multiplier=1).then_inc(selector_step, 1)
            pool.wait_ge(selector_step, 2)
            nc.gpsimd.affine_select(out=selector_f, in_=selector_f, compare_op=ALU.not_equal, fill=1.0,
                                    base=-ROWS, pattern=rows, channel_multiplier=1).then_inc(selector_ready, 1)

            def mask_scores(group, g):
                pool.wait_ge(scores_read, group + 1)
                pool.wait_ge(fill_done, group + 1)
                wait(pool, exps_done, group)
                nc.gpsimd.tensor_tensor(masked_scores[:].rearrange("p s n -> p (s n)"), kept_scores[:], fill[:, g],
                                        ALU.add).then_inc(masked_done, 1)

            def body(r, steps, active):
                first = r * ROUND
                for t in range(steps):
                    if active(t, LAG_SPLIT1):
                        low1(first + (t - LAG_SPLIT1), t)
                    if starts_group(t, LAG_SCORES_READ) and active(t, LAG_SCORES_READ):
                        groups = (t - LAG_SCORES_READ) // PAIRS
                        mask_scores(r * GROUPS_PER_ROUND + groups, groups % GROUPS_PER_ROUND)

            def low1(pair, t):
                b = slot(t, LAG_SPLIT1, HIDDEN1_BUFS)
                pool.wait_ge(high1_done, pair + 1)
                wait(pool, layer2_done, pair - HIDDEN1_BUFS + 1)
                nc.gpsimd.tensor_tensor(hidden1_low[:, b], hidden1[:, b], hidden1_high[:, b].bitcast(F32),
                                        ALU.subtract).then_inc(low1_done, 1)

            rounds(pool, body, LAG_SCORES_READ + 1)

        @block.scalar
        def _(act):
            act.dma_start(all_queries[:], query_t).then_inc(queries_all_loaded, 16)
            for to, src in ((b1_sb[:], b1), (w2_sb[:], w2.rearrange("(a p) h -> p a h", p=P)), (b2_sb[:], b2),
                            (b3_sb[:], b3.to_broadcast([P, 1]))):
                act.dma_start(to, src).then_inc(consts_loaded, 16)
            act.wait_ge(window_cleared, 1)
            for column in (ROWS, 2 * ROWS):
                act.dma_start(w3_window[:, column:column + 1], w3).then_inc(w3_loaded, 16)
            act.wait_ge(consts_loaded, 16 * 4)
            for n in range(BIAS_PARTS):
                for h in range(HALVES):
                    act.wait_ge(bias_product_done, n * HALVES + h + 1)
                    nc.scalar.activation(
                        all_biases[:, n * part_groups:(n + 1) * part_groups, h, :],
                        bias_banks[n][h].rearrange("p (g u) -> p g u", u=GROUP_USERS),
                        ACT.Identity, bias=b1_sb[:, h:h + 1]).then_inc(bias_done, 1)
            act.wait_ge(bias_done, BIAS_PARTS * HALVES)

            def hidden_layer1(pair, t, r):
                b, ps = (t - LAG_HIDDEN1) % HIDDEN1_BUFS, slot(t, LAG_HIDDEN1, 2)
                in_round = (t - LAG_HIDDEN1) % ROUND
                g, at = in_round // PAIRS, in_round % PAIRS
                own_round = r if t >= LAG_HIDDEN1 else r - 1
                very_first = isinstance(own_round, int) and own_round == 0 and g == 0
                biases = all_biases[:, g] if very_first else user_biases[:, g]
                if at == 0 and not very_first:
                    act.wait_ge(biases_loaded[g], (own_round + min(g, 1)) * 16)
                act.wait_ge(layer1_done, pair + 1)
                wait(act, low1_done, pair - HIDDEN1_BUFS + 1)
                for h in range(HALVES):
                    for s in range(2):
                        user = 2 * at + s
                        last = nc.scalar.activation(
                            hidden1[:, b, h, s * N_KEYS:(s + 1) * N_KEYS],
                            layer1_ps[:, ps, h, s * N_KEYS:(s + 1) * N_KEYS],
                            ACT.Relu, bias=biases[:, h, user:user + 1])
                last.then_inc(hidden1_done, 1)

            def high1(pair, t):
                b = slot(t, LAG_SPLIT1, HIDDEN1_BUFS)
                act.wait_ge(hidden1_done, pair + 1)
                wait(act, layer2_done, pair - HIDDEN1_BUFS + 1)
                nc.scalar.copy(hidden1_high[:, b], hidden1[:, b]).then_inc(high1_done, 1)

            def exponentials(group):
                act.wait_ge(top_step, group * 2 + 2)
                wait(act, sums_step, group * 3)
                for s in range(2):
                    last = nc.scalar.activation(exps[:, s], masked_scores[:, s], ACT.Exp,
                                                bias=minus_top[:, s:s + 1], accum_out=exp_sum[:, s:s + 1])
                last.then_inc(exps_done, 1)

            def make_values(group):
                act.wait_ge(sums_step, group * 3 + 3)
                wait(act, probs_done, group)
                for s in range(2):
                    last = nc.scalar.activation(values[:, s], kept_exps[:, s], ACT.Copy, scale=inverse[:, s:s + 1])
                last.then_inc(values_done, 1)

            def body(r, steps, active):
                first = r * ROUND
                for t in range(steps):
                    if active(t, LAG_HIDDEN1):
                        hidden_layer1(first + (t - LAG_HIDDEN1), t, r)
                    if active(t, LAG_SPLIT1):
                        high1(first + (t - LAG_SPLIT1), t)
                    if starts_group(t, LAG_TOP) and active(t, LAG_TOP):
                        exponentials(r * GROUPS_PER_ROUND + (t - LAG_TOP) // PAIRS)
                    if starts_group(t, LAG_VALUES) and active(t, LAG_VALUES):
                        make_values(r * GROUPS_PER_ROUND + (t - LAG_VALUES) // PAIRS)

            rounds(act, body, LAG_VALUES + 1)

        @block.vector
        def _(dve):
            nc.vector.memset(w3_window[:], 0.0).then_inc(window_cleared, 1)
            dve.wait_ge(w1_loaded, 16)
            nc.vector.tensor_tensor(bias_weights[:], w1_sb[:, 0], w1_sb[:, 2], ALU.add)
            nc.vector.tensor_tensor(key_weights[:, 0:H1], w1_sb[:, 1], w1_sb[:, 2], ALU.subtract
                                    ).then_inc(first_weights_ready, 1)
            dve.wait_ge(queries_all_loaded, 16)
            dve.wait_ge(first_weights_ready, 1)

            def finish_constants():
                dve.wait_ge(consts_loaded, 16 * 4)
                nc.vector.tensor_copy(w2_high[:], w2_sb[:]).then_inc(w2_high_ready, 1)
                dve.wait_ge(w2_high_ready, 1)
                nc.vector.tensor_tensor(w2_low[:], w2_sb[:], w2_high[:].bitcast(F32), ALU.subtract)
                dve.wait_ge(selector_ready, 1)
                nc.vector.tensor_reduce(minus_low_row[:], low_table[:].rearrange("p q i -> p (q i)"), AX_X, ALU.add)
                nc.vector.tensor_copy(selector[:], selector_f).then_inc(consts_ready, 1)

            def weights(pair, t, r):
                b = t % WEIGHT_BUFS
                g, at = t // PAIRS, t % PAIRS
                very_first = isinstance(r, int) and g == 0
                queries = all_queries[:, 0:GROUP_USERS] if very_first else user_queries[:, g]
                if at == 0 and not very_first:
                    dve.wait_ge(queries_loaded[g], (r + min(g, 1)) * 16)
                wait(dve, layer1_done, pair - WEIGHT_BUFS + 1)
                for s in range(2):
                    user = 2 * at + s
                    last = nc.vector.scalar_tensor_tensor(
                        out=user_weights[:, b, s], in0=w1_sb[:, 3], scalar=queries[:, user:user + 1],
                        in1=key_weights[:, 0:H1], op0=ALU.mult, op1=ALU.add)
                last.then_inc(weights_ready, 1)

            def hidden_layer2(pair, t, r):
                b = slot(t, LAG_HIDDEN2, HIDDEN2_BUFS)
                dve.wait_ge(layer2_done, pair + 1)
                wait(dve, scores_done, scored(r, t, LAG_HIDDEN2, HIDDEN2_BUFS))
                nc.vector.tensor_scalar(hidden2[:, b], layer2_ps[:, 0:W], b2_sb[:, 0:1], 0.0, ALU.add, ALU.max
                                        ).then_inc(hidden2_done, 1)

            def make_keep(r, g):
                wait(dve, mask_loaded[g], (r + 1) * 16 * TILES)
                nc.vector.tensor_scalar(keep[:, g], mask_int[:, g], 0.0, None, ALU.is_gt).then_inc(keep_done, 1)

            def make_fill(r, g):
                dve.wait_ge(keep_done, r * GROUPS_PER_ROUND + g + 1)
                nc.vector.tensor_scalar(fill[:, g], keep[:, g], -1.0, -MASKED_SCORE, ALU.add, ALU.mult
                                        ).then_inc(fill_done, 1)

            def read_scores(group, g):
                dve.wait_ge(scores_done, (group + 1) * (PAIRS // SCORED))
                wait(dve, masked_done, group)
                nc.vector.scalar_tensor_tensor(out=kept_scores[:], in0=score_ps[:, 0:W], scalar=b3_sb[:, 0:1],
                                               in1=keep[:, g], op0=ALU.add, op1=ALU.mult).then_inc(scores_read, 1)

            def find_top(group, g):
                dve.wait_ge(masked_done, group + 1)
                nc.vector.tensor_reduce(top[:], masked_scores[:], AX_X, ALU.max).then_inc(top_step, 1)

            def negate_top(group, g):
                dve.wait_ge(top_step, group * 2 + 1)
                nc.vector.tensor_scalar(minus_top[:], top[:], -1.0, None, ALU.mult).then_inc(top_step, 1)

            def sums(group, g):
                dve.wait_ge(exps_done, group + 1)
                wait(dve, values_done, group)
                for s in range(2):
                    last = nc.vector.scalar_tensor_tensor(
                        out=kept_exps[:, s], in0=exps[:, s], scalar=1.0, in1=keep[:, g, s * N_KEYS:(s + 1) * N_KEYS],
                        op0=ALU.mult, op1=ALU.mult, accum_out=kept_sum[:, s:s + 1])
                last.then_inc(sums_step, 1)

            def bound_sums(group, g):
                dve.wait_ge(sums_step, group * 3 + 1)
                nc.vector.scalar_tensor_tensor(out=denominator[:], in0=exp_sum[:], scalar=LEAST_DENOMINATOR,
                                               in1=kept_sum[:], op0=ALU.mult, op1=ALU.max).then_inc(sums_step, 1)

            def invert(group, g):
                dve.wait_ge(sums_step, group * 3 + 2)
                nc.vector.reciprocal(inverse[:], denominator[:]).then_inc(sums_step, 1)

            def round_values(group, g):
                dve.wait_ge(values_done, group + 1)
                nc.vector.tensor_copy(values_high[:], values[:].rearrange("p s n -> p (s n)")
                                      ).then_inc(high_probs_done, 1)

            def make_probs(group, g):
                dve.wait_ge(high_probs_done, group + 1)
                wait(dve, spread_done, (group - GROUPS_PER_ROUND + 1) * PAIRS)
                nc.vector.scalar_tensor_tensor(
                    out=probs[:, g], in0=values_high[:].bitcast(F32), scalar=minus_low_row[:, 0:1],
                    in1=values[:].rearrange("p s n -> p (s n)"), op0=ALU.mult, op1=ALU.add).then_inc(probs_done, 1)

            def pool_keys(pair, t, r):
                in_round = (t - LAG_POOL) % ROUND
                g, at = in_round // PAIRS, in_round % PAIRS
                if at == 0:
                    wait(dve, out_stored[g], (r + (0 if t >= LAG_POOL else -1)) * 16)
                dve.wait_ge(spread_done, pair + 1)
                wait(dve, pooled_done, pair - 1)
                bank = spread_bank(r, t - (LAG_POOL - LAG_SPREAD), at)
                for s in range(2):
                    user = 2 * at + s
                    last = nc.vector.scalar_tensor_tensor(
                        out=product[:, at % 2, s], in0=keys[:, in_round, s * N_KEYS:(s + 1) * N_KEYS], scalar=1.0,
                        in1=bank[:, s * N_KEYS:(s + 1) * N_KEYS], op0=ALU.mult, op1=ALU.mult,
                        accum_out=pooled[:, g, user:user + 1])
                last.then_inc(pooled_done, 1)

            def softmax_parts(r, t, active, parts):
                for part, lag in parts:
                    if starts_group(t, lag) and active(t, lag):
                        groups = (t - lag) // PAIRS
                        part(r * GROUPS_PER_ROUND + groups, groups % GROUPS_PER_ROUND)

            def body(r, steps, active):
                first = r * ROUND
                for t in range(steps):
                    if active(t, LAG_POOL):
                        pool_keys(first + (t - LAG_POOL), t, r)
                    softmax_parts(r, t, active, ((find_top, LAG_TOP), (bound_sums, LAG_INVERSE),
                                                 (round_values, LAG_PROBS)))
                    if active(t, 0):
                        weights(first + t, t, r)
                        if t % PAIRS == MASK_STEP:
                            make_keep(r, t // PAIRS)
                        if t == 1 and isinstance(r, int):
                            finish_constants()
                    softmax_parts(r, t, active, ((invert, LAG_INVERSE),))
                    if active(t, LAG_HIDDEN2):
                        hidden_layer2(first + (t - LAG_HIDDEN2), t, r)
                    if active(t, 0) and t % PAIRS == MASK_STEP:
                        make_fill(r, t // PAIRS)
                    softmax_parts(r, t, active, ((read_scores, LAG_SCORES_READ), (negate_top, LAG_TOP),
                                                 (sums, LAG_SUMS), (make_probs, LAG_PROBS)))

            rounds(dve, body, LAG_POOL)

        @block.tensor
        def _(pe):
            pe.wait_ge(first_weights_ready, 1)
            pe.wait_ge(queries_all_loaded, 16)
            part_users = n_users // BIAS_PARTS
            for n in range(BIAS_PARTS):
                for h in range(HALVES):
                    nc.tensor.matmul(bias_banks[n][h], bias_weights[:, h * P:(h + 1) * P],
                                     all_queries[:, n * part_users:(n + 1) * part_users],
                                     start=True, stop=True).then_inc(bias_product_done, 1)

            def layer1(pair, t, r):
                b, ps = (t - LAG_LAYER1) % WEIGHT_BUFS, slot(t, LAG_LAYER1, 2)
                in_round = (t - LAG_LAYER1) % ROUND
                if in_round % CHUNK == 0:
                    wait(pe, keys_loaded[in_round // CHUNK], (r + (1 if t >= LAG_LAYER1 else 0)) * 16)
                pe.wait_ge(weights_ready, pair + 1)
                wait(pe, hidden1_done, pair - 1)
                if isinstance(pair, int) and pair == 1:
                    pe.wait_ge(bias_done, BIAS_PARTS * HALVES)
                for h in range(HALVES):
                    for s in range(2):
                        last = nc.tensor.matmul(layer1_ps[:, ps, h, s * N_KEYS:(s + 1) * N_KEYS],
                                                user_weights[:, b, s, h * P:(h + 1) * P],
                                                keys[:, in_round, s * N_KEYS:(s + 1) * N_KEYS],
                                                start=True, stop=True)
                last.then_inc(layer1_done, 1)

            def layer2(pair, t):
                b = slot(t, LAG_LAYER2, HIDDEN1_BUFS)
                parts = [(w, x, h) for h in range(HALVES) for w, x in
                         ((w2_high, hidden1_high), (w2_low, hidden1_high), (w2_high, hidden1_low))]
                pe.wait_ge(low1_done, pair + 1)
                if isinstance(pair, int) and pair == 0:
                    pe.wait_ge(consts_ready, 1)
                wait(pe, hidden2_done, pair)
                for n, (w, x, h) in enumerate(parts):
                    last = nc.tensor.matmul(layer2_ps[:, 0:W], w[:, h], x[:, b, h],
                                            start=(n == 0), stop=(n == len(parts) - 1))
                last.then_inc(layer2_done, 1)

            def score(pair, t, r):
                at_first = (t - LAG_SCORE) % PAIRS - (SCORED - 1)
                if at_first == 0:
                    wait(pe, scores_read, r * GROUPS_PER_ROUND + (t - LAG_SCORE) // PAIRS)
                pe.wait_ge(hidden2_done, pair + 1)
                if isinstance(pair, int) and pair == SCORED - 1:
                    pe.wait_ge(w3_loaded, 16 * 2)
                for n in range(SCORED):
                    q, row = tile_and_row(at_first + n)
                    b = slot(t, LAG_SCORE + SCORED - 1 - n, HIDDEN2_BUFS)
                    last = nc.tensor.matmul(score_ps[TILE * q:TILE * (q + 1), 0:W],
                                            w3_window[:, ROWS - row:ROWS - row + TILE], hidden2[:, b],
                                            start=(row == 0), stop=(row == ROWS - 1))
                last.then_inc(scores_done, 1)

            def spread(pair, t, r):
                in_round = (t - LAG_SPREAD) % ROUND
                g, at = in_round // PAIRS, in_round % PAIRS
                q, row = tile_and_row(at)
                if at == 0:
                    pe.wait_ge(probs_done, r * GROUPS_PER_ROUND + (t - LAG_SPREAD) // PAIRS + 1)
                bank = spread_bank(r, t, at)
                wait(pe, pooled_done, pair if bank is spread_ps else pair - 3)
                nc.tensor.matmul(bank[:, 0:W], selector[:, row, q], probs[:, g], start=True, stop=True
                                 ).then_inc(spread_done, 1)

            def body(r, steps, active):
                first = r * ROUND
                for t in range(steps):
                    if active(t, LAG_LAYER1):
                        layer1(first + (t - LAG_LAYER1), t, r)
                    if active(t, LAG_LAYER2):
                        layer2(first + (t - LAG_LAYER2), t)
                    if active(t, LAG_SPREAD):
                        spread(first + (t - LAG_SPREAD), t, r)
                    if (t - LAG_SCORE) % SCORED == SCORED - 1 and active(t, LAG_SCORE):
                        score(first + (t - LAG_SCORE), t, r)

            rounds(pe, body, LAG_SPREAD)



def kernel(r_query, r_keys, r_mask, L0_rec_W1, L0_rec_b1, L0_rec_W2, L0_rec_b2, L0_rec_W3, L0_rec_b3):
    import numpy as np
    import concourse.bacc as bacc
    from concourse.bass_utils import run_bass_kernel_spmd

    keys = np.asarray(r_keys)
    n_users, n_keys, d = keys.shape
    chunk_users = 2 * CHUNK
    group_users = 2 * PAIRS
    keys_t = keys.reshape(n_users // chunk_users, chunk_users, n_keys, d).transpose(0, 3, 1, 2)
    masks = np.asarray(r_mask).reshape(n_users // group_users, ROWS, TILES, 2 * n_keys).transpose(0, 2, 1, 3)
    masks = np.concatenate([masks, masks], axis=2)
    arrays = {
        "keys_t": keys_t.reshape(n_users // chunk_users, d, chunk_users * n_keys),
        "query_t": np.asarray(r_query).T,
        "mask": masks,
        "w1": np.asarray(L0_rec_W1),
        "b1": np.asarray(L0_rec_b1).reshape(-1, P).T,
        "w2": np.asarray(L0_rec_W2),
        "b2": np.asarray(L0_rec_b2).reshape(P, 1),
        "w3": np.asarray(L0_rec_W3).reshape(P, 1),
        "b3": np.asarray(L0_rec_b3).reshape(1, 1),
    }
    arrays = {name: np.ascontiguousarray(a) for name, a in arrays.items()}
    nc = bacc.Bacc("TRN2", target_bir_lowering=False, num_devices=1)
    args = [nc.dram_tensor(name, a.shape, mybir.dt.from_np(a.dtype), kind="ExternalInput").ap()
            for name, a in arrays.items()]
    out = nc.dram_tensor("out", (n_users // group_users, d, group_users), F32, kind="ExternalOutput").ap()
    target_attention_kernel(nc, *args, out)
    got = run_bass_kernel_spmd(nc, [arrays], core_ids=[0]).results[0]["out"]
    return np.ascontiguousarray(np.asarray(got).transpose(0, 2, 1)).reshape(n_users, d)
```
